# Optimizing a Trainium2 kernel written in Bass

```python
import numpy as np
import jax
import jax.numpy as jnp

def _softmax(x, axis=-1):
    return jax.nn.softmax(x, axis=axis)

def _gelu(x):
    return jax.nn.gelu(x, approximate=True)

def _silu(x):
    return jax.nn.silu(x)

def _sigmoid(x):
    return jax.nn.sigmoid(x)

def _layernorm(x, axis=-1, eps=1e-05):
    m = jnp.mean(x, axis=axis, keepdims=True)
    v = jnp.var(x, axis=axis, keepdims=True)
    return (x - m) / jnp.sqrt(v + eps)

def _scatter_add(tgt, idx, src, axis=0):
    return tgt.at[idx].add(src)

def _segment_sum(src, seg, n):
    return jax.ops.segment_sum(src, seg, n)
kernel_name = 'mk_decoder_postln_d1_seqx_r4_22a964'

def setup_inputs(seed: int=0):
    np.random.seed(seed)
    _w = jnp.asarray

    def _rec_inputs():
        import jax
        import jax.numpy as jnp
        _rk = jax.random.key(seed)
        x = 7.22e-05 + 1 * jax.random.normal(jax.random.fold_in(_rk, 1), (32, 256, 256), jnp.float32)
        _lenS = 256 - jax.random.randint(jax.random.fold_in(_rk, 7), (32,), 0, max(1, 256 // 4) + 1, jnp.int32)
        _lenS2 = 120 - jax.random.randint(jax.random.fold_in(_rk, 8), (32,), 0, max(1, 120 // 4) + 1, jnp.int32)
        _ctx_1024P = jax.random.normal(jax.random.fold_in(_rk, 11), (32, 16, 256), jnp.float32)
        _ctx_1024c = jax.random.dirichlet(jax.random.fold_in(_rk, 511), 0.3 * jnp.ones((16,), jnp.float32), (32, 120))
        _ctx_1024t = jnp.einsum('bsk,bkd->bsd', _ctx_1024c, _ctx_1024P)
        _ctx_1024t = _ctx_1024t * jax.lax.rsqrt(jnp.mean(jnp.square(_ctx_1024t)) + 1e-12) * 0.953939
        ctx_1024 = 4.13588e-05 + 0.999923 * (_ctx_1024t + 0.3 * jax.random.normal(jax.random.fold_in(_rk, 611), (32, 120, 256), jnp.float32))
        return (x, ctx_1024)
    x, ctx_1024 = _rec_inputs()

    def _L0_attn_setup():
        import jax, jax.numpy as jnp
        import numpy as np
        B, T, C = (2, 512, 256)
        H, L = (16, 72)
        D_HEAD = C // H
        key = jax.random.key(seed)
        ks = jax.random.split(key, 7)
        s = 0.02
        return {'x': jax.random.normal(ks[0], (B, T, C), dtype=jnp.float32), 'latent_w': jax.random.normal(ks[1], (C, L), dtype=jnp.float32) * s, 'latent_b': jax.random.normal(ks[2], (L,), dtype=jnp.float32) * s, 'Wd_w': jax.random.normal(ks[3], (H, C, L), dtype=jnp.float32) * s, 'Wd_b': jax.random.normal(ks[4], (H, L), dtype=jnp.float32) * s, 'out_w': jax.random.normal(ks[5], (H * L, C), dtype=jnp.float32) * s, 'out_b': jax.random.normal(ks[6], (C,), dtype=jnp.float32) * s}
    _L0_attn_all = _L0_attn_setup()
    _L0_attn_in = {k: v for k, v in _L0_attn_all.items() if k in ('latent_w', 'latent_b', 'Wd_w', 'Wd_b', 'out_w', 'out_b')}
    del _L0_attn_all

    def _L0_xattn_setup():
        import jax, jax.numpy as jnp
        import numpy as np
        key = jax.random.key(seed)
        ks = jax.random.split(key, 7)
        B, S, D, H, Dh = (4, 512, 256, 16, 64)
        return {'query_input': jax.random.normal(ks[0], (B, S, D), jnp.float32), 'key_input': jax.random.normal(ks[1], (B, S, D), jnp.float32), 'value_input': jax.random.normal(ks[2], (B, S, D), jnp.float32), 'Wq': jax.random.normal(ks[3], (D, H, Dh), jnp.float32) * 0.03, 'Wk': jax.random.normal(ks[4], (D, H, Dh), jnp.float32) * 0.03, 'Wv': jax.random.normal(ks[5], (D, H, Dh), jnp.float32) * 0.03, 'Wo': jax.random.normal(ks[6], (H, Dh, D), jnp.float32) * 0.03}
    _L0_xattn_all = _L0_xattn_setup()
    _L0_xattn_in = {k: v for k, v in _L0_xattn_all.items() if k in ('Wq', 'Wk', 'Wv', 'Wo')}
    del _L0_xattn_all

    def _L0_ffn_setup():
        import jax, jax.numpy as jnp
        import numpy as np
        B, S, D = (4, 1024, 256)
        E, F_EXP = (16, 512)
        F_C = 2.0
        F_SH = 512
        key = jax.random.key(seed)
        ks = jax.random.split(key, 8)
        s = 0.02
        return {'hidden_states': jax.random.normal(ks[0], (B, S, D), jnp.float32), 'gate_w': jax.random.normal(ks[1], (E, D), jnp.float32) * s, 'Wg': jax.random.normal(ks[2], (E, F_EXP, D), jnp.float32) * s, 'Wu': jax.random.normal(ks[3], (E, F_EXP, D), jnp.float32) * s, 'Wd': jax.random.normal(ks[4], (E, D, F_EXP), jnp.float32) * s, 'Ws_g': jax.random.normal(ks[5], (F_SH, D), jnp.float32) * s, 'Ws_u': jax.random.normal(ks[6], (F_SH, D), jnp.float32) * s, 'Ws_d': jax.random.normal(ks[7], (D, F_SH), jnp.float32) * s}
    _L0_ffn_all = _L0_ffn_setup()
    _L0_ffn_in = {k: v for k, v in _L0_ffn_all.items() if k in ('gate_w', 'Wg', 'Wu', 'Wd', 'Ws_g', 'Ws_u', 'Ws_d')}
    del _L0_ffn_all
    return {'x': x, 'ctx_1024': ctx_1024, 'L0_attn_latent_w': _L0_attn_in['latent_w'], 'L0_attn_latent_b': _L0_attn_in['latent_b'], 'L0_attn_Wd_w': _L0_attn_in['Wd_w'], 'L0_attn_Wd_b': _L0_attn_in['Wd_b'], 'L0_attn_out_w': _L0_attn_in['out_w'], 'L0_attn_out_b': _L0_attn_in['out_b'], 'L0_xattn_Wq': _L0_xattn_in['Wq'], 'L0_xattn_Wk': _L0_xattn_in['Wk'], 'L0_xattn_Wv': _L0_xattn_in['Wv'], 'L0_xattn_Wo': _L0_xattn_in['Wo'], 'L0_ffn_gate_w': _L0_ffn_in['gate_w'], 'L0_ffn_Wg': _L0_ffn_in['Wg'], 'L0_ffn_Wu': _L0_ffn_in['Wu'], 'L0_ffn_Wd': _L0_ffn_in['Wd'], 'L0_ffn_Ws_g': _L0_ffn_in['Ws_g'], 'L0_ffn_Ws_u': _L0_ffn_in['Ws_u'], 'L0_ffn_Ws_d': _L0_ffn_in['Ws_d']}

def reference(x, ctx_1024, L0_attn_latent_w, L0_attn_latent_b, L0_attn_Wd_w, L0_attn_Wd_b, L0_attn_out_w, L0_attn_out_b, L0_xattn_Wq, L0_xattn_Wk, L0_xattn_Wv, L0_xattn_Wo, L0_ffn_gate_w, L0_ffn_Wg, L0_ffn_Wu, L0_ffn_Wd, L0_ffn_Ws_g, L0_ffn_Ws_u, L0_ffn_Ws_d):
    import jax
    import jax.numpy as jnp

    def _L0_attn_ref(x, latent_w, latent_b, Wd_w, Wd_b, out_w, out_b):
        import jax, jax.numpy as jnp
        import numpy as np
        B, T, C = (2, 512, 256)
        H, L = (16, 72)
        D_HEAD = C // H
        b, t, c = x.shape
        h = Wd_w.shape[0]
        d_head = c // h
        Wdkv = x @ latent_w + latent_b
        q = jnp.einsum('btc,hcl->bhtl', x, Wd_w) + Wd_b[None, :, None, :]
        scores = jnp.einsum('bhtl,bsl->bhts', q, Wdkv) / jnp.asarray(np.sqrt(d_head), dtype=x.dtype)
        causal = jnp.tril(jnp.ones((t, t), dtype=bool))
        scores = jnp.where(causal[None, None, :, :], scores, -jnp.inf)
        attn = jax.nn.softmax(scores, axis=-1)
        y = jnp.einsum('bhts,bsl->bhtl', attn, Wdkv)
        z = jnp.transpose(y, (0, 2, 1, 3)).reshape(b, t, h * Wdkv.shape[-1])
        return z @ out_w + out_b

    def _L0_xattn_ref(query_input, key_input, value_input, Wq, Wk, Wv, Wo):
        import jax, jax.numpy as jnp
        import numpy as np
        q = jnp.einsum('bsd,dhk->bshk', query_input, Wq)
        k = jnp.einsum('bsd,dhk->bshk', key_input, Wk)
        v = jnp.einsum('bsd,dhk->bshk', value_input, Wv)
        depth = Wq.shape[-1]
        q = q * depth ** (-0.5)
        logits = jnp.einsum('bthk,bfhk->bhft', k, q)
        weights = jax.nn.softmax(logits, axis=-1)
        ctx = jnp.einsum('bhft,bthk->bfhk', weights, v)
        return jnp.einsum('bfhk,hkd->bfd', ctx, Wo)

    def _L0_ffn_ref(hidden_states, gate_w, Wg, Wu, Wd, Ws_g, Ws_u, Ws_d):
        import jax, jax.numpy as jnp
        import numpy as np
        B, S, D = (4, 1024, 256)
        E, F_EXP = (16, 512)
        F_C = 2.0
        F_SH = 512
        b, s, d = hidden_states.shape
        e = gate_w.shape[0]
        cap = int(s * F_C / e)
        logits = jnp.einsum('bsd,ed->bse', hidden_states, gate_w)
        scores = jax.nn.softmax(logits, axis=-1).transpose(0, 2, 1)
        topk_w, topk_idx = jax.lax.top_k(scores, cap)
        x_tok = jnp.take_along_axis(hidden_states[:, None, :, :], topk_idx[..., None], axis=2)
        g = jnp.einsum('becd,efd->becf', x_tok, Wg)
        u = jnp.einsum('becd,efd->becf', x_tok, Wu)
        h = jax.nn.gelu(g, approximate=False) * u
        eo = jnp.einsum('becf,edf->becd', h, Wd) * topk_w[..., None]
        offs = (jnp.arange(b) * s)[:, None, None]
        flat_idx = (topk_idx + offs).reshape(-1)
        flat = jnp.zeros((b * s, d), hidden_states.dtype)
        flat = flat.at[flat_idx].add(eo.reshape(-1, d))
        out = flat.reshape(b, s, d)
        gs = jnp.einsum('bsd,fd->bsf', hidden_states, Ws_g)
        us = jnp.einsum('bsd,fd->bsf', hidden_states, Ws_u)
        shared = jnp.einsum('bsf,df->bsd', jax.nn.gelu(gs, approximate=False) * us, Ws_d)
        return out + shared
    x = _layernorm(x + _L0_attn_ref(x, L0_attn_latent_w, L0_attn_latent_b, L0_attn_Wd_w, L0_attn_Wd_b, L0_attn_out_w, L0_attn_out_b), axis=-1)
    x = _layernorm(x + _L0_xattn_ref(x, ctx_1024, ctx_1024, L0_xattn_Wq, L0_xattn_Wk, L0_xattn_Wv, L0_xattn_Wo), axis=-1)
    x = _layernorm(x + _L0_ffn_ref(x, L0_ffn_gate_w, L0_ffn_Wg, L0_ffn_Wu, L0_ffn_Wd, L0_ffn_Ws_g, L0_ffn_Ws_u, L0_ffn_Ws_d), axis=-1)
    return x

_drawn_inputs = setup_inputs


def setup_inputs(seed=0):
    import zlib

    import numpy as np

    out = dict(_drawn_inputs(seed))
    spreads = {}
    factors = {'L0_attn_latent_b': 4.507,
     'L0_attn_Wd_w': 6.584,
     'L0_attn_Wd_b': 22.455,
     'L0_attn_out_b': 2.781,
     'L0_xattn_Wq': 2.877,
     'L0_xattn_Wk': 2.884,
     'L0_ffn_gate_w': 8.0,
     'L0_ffn_Wg': 8.0,
     'L0_ffn_Wu': 8.0,
     'L0_ffn_Wd': 8.0,
     'L0_ffn_Ws_g': 8.0,
     'L0_ffn_Ws_u': 8.0,
     'L0_ffn_Ws_d': 8.0}
    for name, (base, spread) in spreads.items():
        noise = np.random.default_rng([zlib.crc32(name.encode()), seed]).standard_normal(out[name].shape)
        drawn = base * np.exp(spread * noise) if base else spread * noise
        out[name] = jnp.asarray(drawn.astype(out[name].dtype))
    for name, factor in factors.items():
        out[name] = (out[name] * factor).astype(out[name].dtype)
    return out
```

```python
from contextlib import ExitStack

import numpy as np

import concourse.bass as bass
from concourse import mybir

F32 = mybir.dt.float32
F32R = mybir.dt.float32r
BF16 = mybir.dt.bfloat16
U32 = mybir.dt.uint32
ALU = mybir.AluOpType
ACT = mybir.ActivationFunctionType
AXIS = mybir.AxisListType

P = 128
B, T, C = 32, 256, 256
H, L = 16, 72
S, DH = 120, 64
E, F = 16, 512
CAP = int(T * 2.0 / E)
KC = C // P
TT = T // P
NP = H // 2
BODY = 2 * NP
BODIES = B // 2
RING = 4
FT = F // P
KS = E * CAP // P
GB = P // E
NG = B // GB
REST = 2 * L - P
AT = 96
EPS = 1e-5
MASKED = -3e38
SELF_SCALE = float(C // H) ** -0.5
CROSS_SCALE = float(DH) ** -0.5


def need(eng, sem, count):
    if not isinstance(count, int) or count > 0:
        eng.wait_ge(sem, count)


def need_alone(eng, sem, count, spare):
    if not isinstance(count, int) or count > 0:
        eng.wait_ge(sem, count)
        eng.sem_inc(spare, 1)


def upto(J, g, per=1, more=0):
    return J * (BODY * per) + (per * (g + 1) + more)


def upto_seq(J, b, per=1, more=0):
    return J * (2 * per) + (per * (b + 1) + more)


def at_most(count, most):
    return min(count, most) if isinstance(count, int) else count


def step_exists(J, g):
    return not isinstance(J, int) or 0 <= BODY * J + g < B * NP


def seq_exists(J, b):
    return not isinstance(J, int) or 0 <= 2 * J + b < B


def over_bodies(eng, body, first, end, after):
    for J in range(first):
        body(J)
    with eng.Fori(first, end) as J:
        body(J)
    for J in range(end, after):
        body(J)


def three(pe, out, stat_hi, stat_lo, mov_hi, mov_lo, start, stop):
    pe.matmul(out, stat_hi, mov_hi, start=start, stop=False, skip_group_check=True)
    pe.matmul(out, stat_hi, mov_lo, start=False, stop=False, skip_group_check=True)
    return pe.matmul(out, stat_lo, mov_hi, start=False, stop=stop, skip_group_check=True)


def two(pe, out, stat_hi, stat_lo, mov_hi, mov_lo, start, stop):
    pe.matmul(out, stat_hi, mov_hi, start=start, stop=False, skip_group_check=True)
    rows = slice(0, AT + REST)
    return pe.matmul(out, stat_lo[rows], mov_lo[rows], start=False, stop=stop, skip_group_check=True)


class Alloc:

    def __init__(self, nc, ctx, tag):
        self.nc, self.ctx, self.tag, self.sems = nc, ctx, tag, []
        ctx.callback(self.clear)

    def sb(self, name, shape, dt=F32):
        return self.ctx.enter_context(self.nc.sbuf_tensor(f"{self.tag}_{name}", shape, dt))

    def split(self, name, shape):
        return self.sb(name + "_hi", shape, F32R), self.sb(name + "_lo", shape, F32R)

    def sem(self, name):
        self.sems.append(self.nc.alloc_semaphore(name=f"{self.tag}_{name}"))
        return self.sems[-1]

    def clear(self):
        self.nc.clear_and_free_semaphores(self.sems)
        self.nc.all_engine_barrier()


def f32(ap):
    return ap.bitcast(F32)




def self_attention(nc, bank, ident, d):
    with ExitStack() as ctx:
        al = Alloc(nc, ctx, "sa")
        wd_hi, wd_lo = al.split("wd", [P, KC, H * P])
        lw_hi, lw_lo = al.split("lw", [P, KC, P])
        ow = al.sb("ow", [P, 2, H * C], F32R)
        qbias, lbias, obias = al.sb("qbias", [P, H]), al.sb("lbias", [P, 1]), al.sb("obias", [P, C])
        ones, minus_low = al.sb("ones", [P, 1]), al.sb("minus_low", [P, 1])
        mask = al.sb("mask", [P, 3, P])
        half = al.sb("half", [P, TT])
        xT_raw = al.sb("xT_raw", [P, 2, KC, T])
        x_hi, x_lo = al.split("xT", [P, 2, KC, T])
        x_res = al.sb("x_res", [P, 2, TT, C])
        kvT = al.sb("kvT", [P, T])
        kvT_a, kvT_b = al.sb("kvT_a", [P, 2, T], F32R), al.sb("kvT_b", [P, 2, T], F32R)
        kv_hi, kv_lo = al.split("kv", [P, 2, TT, P])
        q_hi, q_lo = al.split("q", [P, RING, 2, T])
        shift = al.sb("shift", [P, RING, 4])
        total = al.sb("total", [P, RING, 4])
        inverse = al.sb("inverse", [P, RING, 4])
        res = al.sb("res", [P, TT, C])
        stats, meanvar = al.sb("stats", [P, TT, 6]), al.sb("meanvar", [P, TT, 2])
        var_eps, rstd = al.sb("var_eps", [P, TT]), al.sb("rstd", [P, TT])
        x1 = al.sb("x1", [P, 2, TT, C])
        with ExitStack() as first:
            wd_raw = first.enter_context(nc.sbuf_tensor("sa_wd_raw", [P, KC, H * P], F32))
            lw_raw = first.enter_context(nc.sbuf_tensor("sa_lw_raw", [P, KC, P], F32))
            ow_raw = first.enter_context(nc.sbuf_tensor("sa_ow_raw", [P, 2, H * C], F32))
        prob = al.sb("prob", [P, RING, 2, 3 * P])
        pT_hi, pT_lo = al.split("pT", [P, RING, 2, 3 * P])
        y_hi, y_lo = al.split("y", [P, RING, 2, T])

        Q, SC, TR, PV, O, KV = bank[0], bank[1:3], bank[3:5], bank[5], bank[6], bank[7]

        w_in, w_hi, w_lo, const = al.sem("w_in"), al.sem("w_hi"), al.sem("w_lo"), al.sem("const")
        ow_in, owhi_done, ow_done = al.sem("ow_in"), al.sem("owhi_done"), al.sem("ow_done")
        xT_in = [al.sem(f"xT_in{i}") for i in range(2)]
        res_in = [al.sem(f"res_in{i}") for i in range(2)]
        x1_out = [al.sem(f"x1_out{i}") for i in range(2)]
        xhi_done, xlo_done, xres_done = al.sem("xhi_done"), al.sem("xlo_done"), al.sem("xres_done")
        kvT_mm, kvT_done, kvTb_done = al.sem("kvT_mm"), al.sem("kvT_done"), al.sem("kvTb_done")
        kv_tr, kvhi_done, kv_done = al.sem("kv_tr"), al.sem("kvhi_done"), al.sem("kv_done")
        qdup_done, ydup_done = al.sem("qdup_done"), al.sem("ydup_done")
        q_mm, qhi_done, qlo_done = al.sem("q_mm"), al.sem("qhi_done"), al.sem("qlo_done")
        s_mm, s_read, exp_done = al.sem("s_mm"), al.sem("s_read"), al.sem("exp_done")
        inv_done, p_done = al.sem("inv_done"), al.sem("p_done")
        p_tr, pThi_done, pTlo_done = al.sem("p_tr"), al.sem("pThi_done"), al.sem("pTlo_done")
        pv_mm, yhi_done, ylo_done = al.sem("pv_mm"), al.sem("yhi_done"), al.sem("ylo_done")
        o_mm, o_read = al.sem("o_mm"), al.sem("o_read")
        st_done, mv_done, ve_done, rstd_done, x1_done = (
            al.sem("st_done"), al.sem("mv_done"), al.sem("ve_done"), al.sem("rstd_done"), al.sem("x1_done"))
        spare_dve, spare_pool = al.sem("spare_dve"), al.sem("spare_pool")

        QL, SL, IL, TL, PL, OL = 1, 3, 4, 5, 7, 9
        KV_MM, KV_TR, RES, NORM = 2, 4, 12, 17

        OW_PARTS = 4
        OW_COLS = 2 * H * C // OW_PARTS
        ow_flat, ow_raw_flat = ow[:].rearrange("p a n -> p (a n)"), ow_raw[:].rearrange("p a n -> p (a n)")

        block = ctx.enter_context(nc.Block())

        @block.sync
        def _(sp):
            sp.dma_start(wd_raw[:], d["wd"].rearrange("(k p) n -> p k n", p=P)).then_inc(w_in, 16)
            sp.dma_start(lw_raw[:], d["lw"].rearrange("(k p) n -> p k n", p=P)).then_inc(w_in, 16)
            sp.dma_start(qbias[:], d["qbias"]).then_inc(w_in, 16)
            sp.dma_start(lbias[:], d["lbias"]).then_inc(w_in, 16)

            def body(J):
                for i in range(2):
                    if seq_exists(J, i):
                        need(sp, xlo_done, upto_seq(J, i - 2))
                        sp.dma_start(xT_raw[:, i], d["xT"][J * 2 + i].rearrange("(k p) t -> p k t", p=P)).then_inc(xT_in[i], 16)
                        need(sp, o_read, upto_seq(J, i - 2))
                        sp.dma_start(x_res[:, i], d["x"][J * 2 + i].rearrange("(t p) c -> p t c", p=P)).then_inc(res_in[i], 16)
                    if isinstance(J, int) and J == 0 and i == 1:
                        sp.dma_start(ow_raw[:, 0], d["ow_a"]).then_inc(ow_in, 16)
                        sp.dma_start(ow_raw[:, 1], d["ow_b"]).then_inc(ow_in, 16)
                        sp.dma_start(obias[:], d["obias"]).then_inc(ow_in, 16)
                    if seq_exists(J, i - 3):
                        k = (i - 3) % 2
                        need(sp, x1_done, upto_seq(J, i - 3))
                        sp.dma_start(d["x1"][J * 2 + (i - 3)].rearrange("(t p) c -> p t c", p=P), x1[:, k]).then_inc(x1_out[k], 16)

            over_bodies(sp, body, 2, BODIES, BODIES + 2)
            for i in range(2):
                sp.wait_ge(x1_out[i], 16 * BODIES)

        @block.gpsimd
        def _(pool):
            pool.memset(mask[:], 0.0).then_inc(const, 1)
            pool.memset(half[:], -0.5).then_inc(const, 1)
            pool.memset(minus_low[:], -1.0).then_inc(const, 1)
            pool.memset(f32(kvT_b[:]), 0.0).then_inc(const, 1)
            pool.wait_ge(const, 4)
            pool.affine_select(out=minus_low[:], in_=minus_low[:], compare_op=ALU.is_ge, fill=0.0, base=-L,
                               pattern=[[0, 1]], channel_multiplier=1).then_inc(const, 1)
            pool.affine_select(out=mask[:, 0], in_=mask[:, 0], compare_op=ALU.is_ge, fill=MASKED, base=0,
                               pattern=[[-1, P]], channel_multiplier=1).then_inc(const, 1)
            pool.affine_select(out=mask[:, 2], in_=mask[:, 2], compare_op=ALU.is_ge, fill=MASKED, base=0,
                               pattern=[[-1, P]], channel_multiplier=1).then_inc(const, 1)
            pool.wait_ge(const, 7)
            pool.wait_ge(ow_in, 48)

            def body(J):
                for m in range(BODY):
                    if m % NP == RES % NP and seq_exists(J, (m - RES) // NP):
                        b = (m - RES) // NP
                        i = b % 2
                        need(pool, res_in[i], J * 16 + 16 * (b // 2 + 1))
                        for t in range(TT):
                            pool.tensor_tensor(x_res[:, i, t], x_res[:, i, t], obias[:], ALU.add).then_inc(xres_done, 1)
                        need(pool, xres_done, upto_seq(J, b, TT))
                    g = m - IL
                    if step_exists(J, g):
                        r = g % RING
                        need_alone(pool, inv_done, upto(J, g), spare_pool)
                        for hh in range(2):
                            pool.tensor_scalar(prob[:, r, hh, 0:P], prob[:, r, hh, 0:P], inverse[:, r, 2 * hh:2 * hh + 1],
                                               1.0, ALU.mult, ALU.mult)
                            pool.tensor_scalar(prob[:, r, hh, P:3 * P], prob[:, r, hh, P:3 * P],
                                               inverse[:, r, 2 * hh + 1:2 * hh + 2], 1.0, ALU.mult, ALU.mult).then_inc(p_done, 1)
                    g = m - QL
                    if step_exists(J, g):
                        r = g % RING
                        need(pool, p_done, at_most(upto(J, m - IL, 2), 2 * B * NP))
                        need_alone(pool, qhi_done, upto(J, g, 2), spare_pool)
                        pool.tensor_scalar(q_lo[AT:AT + REST, r], f32(q_hi[0:REST, r]), 1.0, 1.0, ALU.mult, ALU.mult).then_inc(qdup_done, 1)
                        need(pool, qdup_done, upto(J, g))
                    g = m - PL
                    if step_exists(J, g):
                        r = g % RING
                        need(pool, p_done, at_most(upto(J, m - IL, 2), 2 * B * NP))
                        need_alone(pool, yhi_done, upto(J, g), spare_pool)
                        pool.tensor_scalar(y_lo[AT:AT + REST, r], f32(y_hi[0:REST, r]), 1.0, 1.0, ALU.mult, ALU.mult).then_inc(ydup_done, 1)
                        need(pool, ydup_done, upto(J, g))
                    if m % NP == NORM % NP and seq_exists(J, (m - NORM) // NP):
                        need(pool, ve_done, upto_seq(J, (m - NORM) // NP))
                        pool.tensor_tensor(rstd[:], var_eps[:], half[:], ALU.pow).then_inc(rstd_done, 1)

            over_bodies(pool, body, 1, BODIES, BODIES + 1)

        @block.tensor
        def _(pe):
            first_use = {QL: (w_lo, 2), OL: (ow_done, OW_PARTS)}

            def body(J):
                for m in range(BODY):
                    if isinstance(J, int) and J == 0 and m in first_use:
                        pe.wait_ge(*first_use[m])
                    if m % NP == KV_MM and seq_exists(J, (m - KV_MM) // NP):
                        b = (m - KV_MM) // NP
                        need(pe, xlo_done, upto_seq(J, b))
                        need(pe, kv_done, upto_seq(J, b - 1))
                        for k in range(KC):
                            mm = three(pe, KV[:, 0:T], lw_hi[:, k], lw_lo[:, k], x_hi[:, b % 2, k], x_lo[:, b % 2, k],
                                       k == 0, k == KC - 1)
                        mm.then_inc(kvT_mm, 1)
                    g = m - SL
                    if step_exists(J, g):
                        r, b = g % RING, (g // NP) % 2
                        if g % NP == 0:
                            need(pe, kvTb_done, upto_seq(J, g // NP, 2))
                        need(pe, qdup_done, upto(J, g))
                        for hh in range(2):
                            need(pe, qlo_done, upto(J, g, 2, hh - 1))
                            need(pe, s_read, upto(J, g - 1, 4, 2 * hh - 2))
                            for t in range(TT):
                                tk = slice(t * P, t * P + P)
                                mm = two(pe, SC[hh][:, t * T:t * T + T], q_hi[:, r, hh, tk], q_lo[:, r, hh, tk],
                                         kvT_a[:, b], kvT_b[:, b], True, True)
                            mm.then_inc(s_mm, 1)
                    g = m - QL
                    if step_exists(J, g):
                        b, p = (g // NP) % 2, g % NP
                        if p == 0:
                            need(pe, xlo_done, upto_seq(J, g // NP))
                        need(pe, qlo_done, upto(J, g - 1, 2))
                        for hh in range(2):
                            w = slice((2 * p + hh) * P, (2 * p + hh + 1) * P)
                            for k in range(KC):
                                mm = three(pe, Q[:, hh * T:hh * T + T], wd_hi[:, k, w], wd_lo[:, k, w],
                                           x_hi[:, b, k], x_lo[:, b, k], k == 0, k == KC - 1)
                        mm.then_inc(q_mm, 1)
                    g = m - PL
                    if step_exists(J, g):
                        r, b = g % RING, (g // NP) % 2
                        if g % NP == 0:
                            need(pe, kv_done, upto_seq(J, g // NP))
                        need(pe, pTlo_done, upto(J, g, 2))
                        need(pe, ylo_done, upto(J, g - 1))
                        out = PV[:].rearrange("l (h t) -> l h t", h=2)
                        three(pe, out, kv_hi[:, b, 0], kv_lo[:, b, 0], pT_hi[:, r, :, 0:T], pT_lo[:, r, :, 0:T], True, False)
                        three(pe, out[:, :, P:T], kv_hi[:, b, 1], kv_lo[:, b, 1], pT_hi[:, r, :, T:3 * P],
                              pT_lo[:, r, :, T:3 * P], False, True).then_inc(pv_mm, 1)
                    g = m - TL
                    if step_exists(J, g):
                        r = g % RING
                        for hh in range(2):
                            need(pe, p_done, upto(J, g, 2, hh - 1))
                            need(pe, pTlo_done, upto(J, g - 1, 2, hh - 1))
                            for n in range(3):
                                mm = pe.transpose(TR[hh][:, n * P:n * P + P], prob[:, r, hh, n * P:n * P + P], ident[:])
                            mm.then_inc(p_tr, 1)
                    if m % NP == KV_TR and seq_exists(J, (m - KV_TR) // NP):
                        b = (m - KV_TR) // NP
                        need(pe, kvT_done, upto_seq(J, b, 3))
                        for t in range(TT):
                            mm = pe.transpose(KV[:, T + t * P:T + t * P + P], kvT[:, t * P:t * P + P], ident[:])
                        mm.then_inc(kv_tr, 1)
                    g = m - OL
                    if step_exists(J, g):
                        r, p = g % RING, g % NP
                        need(pe, ylo_done, upto(J, g))
                        need(pe, ydup_done, upto(J, g))
                        if p == 0:
                            need(pe, o_read, upto_seq(J, g // NP - 1))
                        for hh in range(2):
                            w = slice((2 * p + hh) * C, (2 * p + hh + 1) * C)
                            for t in range(TT):
                                tk = slice(t * P, t * P + P)
                                mm = two(pe, O[:, t * C:t * C + C], y_hi[:, r, hh, tk], y_lo[:, r, hh, tk], ow[:, 0, w],
                                         ow[:, 1, w], p == 0 and hh == 0 and t == 0, p == NP - 1 and hh == 1)
                        mm.then_inc(o_mm, 1)

            over_bodies(pe, body, 1, BODIES, BODIES + 1)

        @block.scalar
        def _(act):
            act.wait_ge(w_in, 64)
            act.activation(wd_hi[:], wd_raw[:], ACT.Copy).then_inc(w_hi, 1)
            act.activation(lw_hi[:], lw_raw[:], ACT.Copy).then_inc(w_hi, 1)

            def body(J):
                for m in range(BODY):
                    if m % NP == 0 and seq_exists(J, m // NP):
                        b = m // NP
                        need(act, xT_in[b], J * 16 + 16)
                        need(act, q_mm, upto(J, (b - 1) * NP - 1))
                        act.activation(x_hi[:, b], xT_raw[:, b], ACT.Copy).then_inc(xhi_done, 1)
                    if m % NP == KV_MM and seq_exists(J, (m - KV_MM) // NP):
                        b = (m - KV_MM) // NP
                        need(act, kvT_mm, upto_seq(J, b))
                        need(act, kv_tr, upto_seq(J, b - 1))
                        need(act, kvTb_done, upto_seq(J, b - 1, 2))
                        act.activation(kvT[:], KV[:, 0:T], ACT.Identity, bias=lbias[:, 0:1]).then_inc(kvT_done, 1)
                        need(act, s_mm, upto(J, (b - 1) * NP - 1, 2))
                        act.activation(kvT_a[:, b % 2], KV[:, 0:T], ACT.Identity, bias=lbias[:, 0:1]).then_inc(kvT_done, 1)
                        act.activation(kvT_b[0:L, b % 2], KV[0:L, 0:T], ACT.Identity, bias=lbias[0:L, 0:1]).then_inc(kvT_done, 1)
                    g = m - QL
                    if step_exists(J, g):
                        r, p = g % RING, g % NP
                        need(act, q_mm, upto(J, g))
                        need(act, s_mm, upto(J, g - RING, 2))
                        for hh in range(2):
                            h = 2 * p + hh
                            act.activation(q_hi[:, r, hh], Q[:, hh * T:hh * T + T], ACT.Identity,
                                           bias=qbias[:, h:h + 1]).then_inc(qhi_done, 1)
                    g = m - PL
                    if step_exists(J, g):
                        r = g % RING
                        need(act, pv_mm, upto(J, g))
                        need(act, o_mm, upto(J, g - RING))
                        act.activation(y_hi[:, r].rearrange("l h t -> l (h t)"), PV[:], ACT.Copy).then_inc(yhi_done, 1)
                    g = m - TL
                    if step_exists(J, g):
                        r = g % RING
                        for hh in range(2):
                            need(act, p_tr, upto(J, g, 2, hh - 1))
                            if hh == 0:
                                need(act, pv_mm, upto(J, g - RING))
                            act.activation(pT_hi[:, r, hh], TR[hh][:, 0:3 * P], ACT.Copy).then_inc(pThi_done, 1)
                    if m % NP == KV_TR and seq_exists(J, (m - KV_TR) // NP):
                        b = (m - KV_TR) // NP
                        need(act, kv_tr, upto_seq(J, b))
                        need(act, pv_mm, upto(J, (b - 1) * NP - 1))
                        act.activation(kv_hi[:, b % 2].rearrange("p t l -> p (t l)"), KV[:, T:T + TT * P],
                                       ACT.Copy).then_inc(kvhi_done, 1)
                    g = m - SL
                    if step_exists(J, g):
                        r = g % RING
                        for hh in range(2):
                            for t in range(TT):
                                n = 2 * hh + t
                                need(act, s_read, upto(J, g, 4, n - 3))
                                cols = slice(0, P) if t == 0 else slice(P, 3 * P)
                                act.activation(prob[:, r, hh, cols], prob[:, r, hh, cols], ACT.Exp, bias=shift[:, r, n:n + 1],
                                               scale=-1.0, accum_out=total[:, r, n:n + 1]).then_inc(exp_done, 1)
                    if isinstance(J, int) and J == 0 and m < OW_PARTS:
                        if m == 0:
                            act.wait_ge(ow_in, 48)
                        part = slice(m * OW_COLS, (m + 1) * OW_COLS)
                        act.activation(ow_flat[:, part], ow_raw_flat[:, part], ACT.Copy).then_inc(owhi_done, 1)

            over_bodies(act, body, 1, BODIES, BODIES + 1)

        @block.vector
        def _(dve):
            for n, (lo, hi, raw) in enumerate(((wd_lo, wd_hi, wd_raw), (lw_lo, lw_hi, lw_raw))):
                dve.wait_ge(w_hi, n + 1)
                dve.tensor_tensor(lo[:], raw[:], f32(hi[:]), ALU.subtract).then_inc(w_lo, 1)
            dve.wait_ge(const, 7)

            def body(J):
                for m in range(BODY):
                    if m % NP == 0 and seq_exists(J, m // NP):
                        b = m // NP
                        need(dve, xhi_done, upto_seq(J, b))
                        dve.tensor_tensor(x_lo[:, b], xT_raw[:, b], f32(x_hi[:, b]), ALU.subtract).then_inc(xlo_done, 1)
                    if m % NP == KV_MM and seq_exists(J, (m - KV_MM) // NP):
                        b = (m - KV_MM) // NP
                        need(dve, kvT_done, upto_seq(J, b, 3))
                        dve.tensor_tensor(kvT_b[AT:AT + REST, b % 2], kvT[0:REST, :], f32(kvT_b[0:REST, b % 2]),
                                          ALU.subtract).then_inc(kvTb_done, 1)
                        dve.scalar_tensor_tensor(out=kvT_a[:, b % 2], in0=f32(kvT_a[:, b % 2]), scalar=minus_low[:, 0:1], in1=kvT[:],
                                                 op0=ALU.mult, op1=ALU.add).then_inc(kvTb_done, 1)
                    if m % NP == NORM % NP and seq_exists(J, (m - NORM) // NP):
                        b = (m - NORM) // NP
                        need(dve, o_mm, upto(J, (b + 1) * NP - 1))
                        need(dve, xres_done, upto_seq(J, b, TT))
                        dve.tensor_tensor(res[:].rearrange("p t c -> p (t c)"), O[:, 0:TT * C],
                                          x_res[:, b % 2].rearrange("p t c -> p (t c)"), ALU.add).then_inc(o_read, 1)
                    g = m - SL
                    if step_exists(J, g):
                        r = g % RING
                        need(dve, p_tr, upto(J, g - RING, 2))
                        for hh in range(2):
                            need_alone(dve, s_mm, upto(J, g, 2, hh - 1), spare_dve)
                            for t in range(TT):
                                n = 2 * hh + t
                                cols = slice(0, P) if t == 0 else slice(P, 3 * P)
                                dve.tensor_tensor_reduce(
                                    out=prob[:, r, hh, cols], in0=SC[hh][:, t * T:t * T + (t + 1) * P],
                                    in1=mask[:].rearrange("p a s -> p (a s)")[:, cols], scale=-SELF_SCALE, scalar=-MASKED,
                                    op0=ALU.add, op1=ALU.min, accum_out=shift[:, r, n:n + 1]).then_inc(s_read, 1)
                    g = m - IL
                    if step_exists(J, g):
                        r = g % RING
                        need(dve, exp_done, upto(J, g, 4))
                        dve.reciprocal(inverse[:, r], total[:, r]).then_inc(inv_done, 1)
                    g = m - QL
                    if step_exists(J, g):
                        r, p = g % RING, g % NP
                        need(dve, qhi_done, upto(J, g, 2))
                        for hh in range(2):
                            h = 2 * p + hh
                            dve.scalar_tensor_tensor(out=q_lo[0:AT, r, hh], in0=Q[0:AT, hh * T:hh * T + T], scalar=qbias[0:AT, h:h + 1],
                                                     in1=f32(q_hi[0:AT, r, hh]), op0=ALU.add, op1=ALU.subtract).then_inc(qlo_done, 1)
                    g = m - PL
                    if step_exists(J, g):
                        r = g % RING
                        need(dve, yhi_done, upto(J, g))
                        dve.tensor_tensor(y_lo[0:AT, r].rearrange("l h t -> l (h t)"), PV[0:AT, :],
                                          f32(y_hi[0:AT, r].rearrange("l h t -> l (h t)")), ALU.subtract).then_inc(ylo_done, 1)
                    g = m - TL
                    if step_exists(J, g):
                        r = g % RING
                        for hh in range(2):
                            need(dve, pThi_done, upto(J, g, 2, hh - 1))
                            dve.tensor_tensor(pT_lo[:, r, hh], TR[hh][:, 0:3 * P], f32(pT_hi[:, r, hh]),
                                              ALU.subtract).then_inc(pTlo_done, 1)
                    if m % NP == KV_TR and seq_exists(J, (m - KV_TR) // NP):
                        b = (m - KV_TR) // NP
                        need(dve, kvhi_done, upto_seq(J, b))
                        dve.tensor_tensor(kv_lo[:, b % 2].rearrange("p t l -> p (t l)"), KV[:, T:T + TT * P],
                                          f32(kv_hi[:, b % 2].rearrange("p t l -> p (t l)")), ALU.subtract).then_inc(kv_done, 1)
                    if m % NP == (NORM + 1) % NP and seq_exists(J, (m - NORM - 1) // NP):
                        b = (m - NORM - 1) // NP
                        need(dve, rstd_done, upto_seq(J, b))
                        need(dve, x1_out[b % 2], J * 16 + 16 * (b // 2))
                        for t in range(TT):
                            ins = dve.tensor_scalar(x1[:, b % 2, t], res[:, t], meanvar[:, t, 0:1], rstd[:, t:t + 1],
                                                    ALU.subtract, ALU.mult)
                        ins.then_inc(x1_done, 1)
                    if m % NP == NORM % NP and seq_exists(J, (m - NORM) // NP):
                        b = (m - NORM) // NP
                        need(dve, o_read, upto_seq(J, b))
                        for t in range(TT):
                            dve.bn_stats(stats[:, t], res[:, t]).then_inc(st_done, 1)
                        need_alone(dve, st_done, upto_seq(J, b, TT), spare_dve)
                        for t in range(TT):
                            dve.bn_aggr(meanvar[:, t], stats[:, t]).then_inc(mv_done, 1)
                        need(dve, mv_done, upto_seq(J, b, TT))
                        dve.tensor_scalar(var_eps[:], meanvar[:, :, 1], EPS, None, ALU.add).then_inc(ve_done, 1)
                    if isinstance(J, int) and J == 0 and m < OW_PARTS:
                        part = slice(m * OW_COLS, (m + 1) * OW_COLS)
                        need(dve, owhi_done, m + 1)
                        dve.scalar_tensor_tensor(out=ow_flat[:, part], in0=f32(ow_flat[:, part]), scalar=minus_low[:, 0:1],
                                                 in1=ow_raw_flat[:, part], op0=ALU.mult, op1=ALU.add).then_inc(ow_done, 1)

            over_bodies(dve, body, 1, BODIES, BODIES + 1)




def cross_attention(nc, bank, ident, logits, d):
    with ExitStack() as ctx:
        al = Alloc(nc, ctx, "ca")
        names = ("wv", "wq", "wk", "wo")
        shapes = {"wq": [P, KC, H * DH], "wk": [P, KC, H * DH], "wv": [P, KC, H * DH], "wo": [P, NP, C]}
        w = {n: al.split(n, shapes[n]) for n in names}
        gate_hi, gate_lo = al.split("gate", [P, KC, E])
        gate_raw = al.sb("gate_raw", [P, KC, E])
        half = al.sb("half", [P, TT])
        x_raw = al.sb("x_raw", [P, 2, TT, C])
        x_res = al.sb("x_res", [P, TT, C])
        xT_hi, xT_lo = al.split("xT", [P, 2, KC, T])
        cT_raw = al.sb("cT_raw", [P, KC, 2, S])
        cT_hi, cT_lo = al.split("cT", [P, KC, 2, S])
        q_hi, q_lo = al.split("q", [P, RING, T])
        prob = al.sb("prob", [P, RING, TT, 2, S])
        shift = al.sb("shift", [P, RING, TT * 2])
        total = al.sb("total", [P, RING, TT * 2])
        inverse = al.sb("inverse", [P, RING, TT * 2])
        pT_hi, pT_lo = al.split("pT", [S, RING, 2, T])
        c_hi, c_lo = al.split("c", [P, RING, T])
        res = al.sb("res", [P, TT, C])
        stats, meanvar = al.sb("stats", [P, TT, 6]), al.sb("meanvar", [P, TT, 2])
        var_eps, rstd = al.sb("var_eps", [P, TT]), al.sb("rstd", [P, TT])
        x2 = al.sb("x2", [P, 2, TT, C])
        x2T_hi, x2T_lo = al.split("x2T", [P, KC, T])
        with ExitStack() as first:
            raw = first.enter_context(nc.sbuf_tensor("ca_raw", [P, len(names), KC * H * DH], F32))
        k_hi, k_lo = al.split("k", [P, 2, NP, 2 * S])
        v_hi, v_lo = al.split("v", [S, 2, NP, 3 * DH])

        SC, QK, TR, CX, O, XT, M = bank[0:2], *bank[2:8]
        Q, K = QK[:, 0:T], QK[:, T:T + 2 * S]

        w_in = [al.sem(f"{n}_in") for n in names]
        w_hi, w_lo, const = al.sem("w_hi"), al.sem("w_lo"), al.sem("const")
        gate_in = al.sem("gate_in")
        x_in = [al.sem(f"x_in{i}") for i in range(2)]
        c_in, res_in = al.sem("c_in"), al.sem("res_in")
        x2_out = [al.sem(f"x2_out{i}") for i in range(2)]
        chi_done, clo_done = al.sem("chi_done"), al.sem("clo_done")
        x_tr, xThi_done, xTlo_done = al.sem("x_tr"), al.sem("xThi_done"), al.sem("xTlo_done")
        v_mm, vhi_done, vlo_done = al.sem("v_mm"), al.sem("vhi_done"), al.sem("vlo_done")
        k_mm, khi_done, klo_done = al.sem("k_mm"), al.sem("khi_done"), al.sem("klo_done")
        q_mm, qhi_done, qlo_done = al.sem("q_mm"), al.sem("qhi_done"), al.sem("qlo_done")
        s_mm, max_done, exp_done = al.sem("s_mm"), al.sem("max_done"), al.sem("exp_done")
        inv_done, p_done = al.sem("inv_done"), al.sem("p_done")
        p_tr, pThi_done, pTlo_done = al.sem("p_tr"), al.sem("pThi_done"), al.sem("pTlo_done")
        cx_mm, cxhi_done, cxlo_done = al.sem("cx_mm"), al.sem("cxhi_done"), al.sem("cxlo_done")
        o_mm, o_read = al.sem("o_mm"), al.sem("o_read")
        st_done, mv_done, ve_done, rstd_done, x2_done = (
            al.sem("st_done"), al.sem("mv_done"), al.sem("ve_done"), al.sem("rstd_done"), al.sem("x2_done"))
        x2_tr, x2Thi_done, x2Tlo_done = al.sem("x2_tr"), al.sem("x2Thi_done"), al.sem("x2Tlo_done")
        g_mm, g_done = al.sem("g_mm"), al.sem("g_done")
        spare_dve, spare_pool, spare_act = al.sem("spare_dve"), al.sem("spare_pool"), al.sem("spare_act")

        QL, SL, IL, TL, CL, OL = 2, 4, 5, 6, 8, 10
        NORM, X2T, GATE = 18, 20, 21

        block = ctx.enter_context(nc.Block())

        @block.sync
        def _(sp):
            for n, name in enumerate(names):
                src = d[name].rearrange("(k p) n -> p k n", p=P) if name != "wo" else d[name].rearrange("p (k n) -> p k n", k=NP)
                sp.dma_start(raw[:, n].rearrange("p (k n) -> p k n", k=shapes[name][1]), src).then_inc(w_in[n], 16)
            sp.dma_start(gate_raw[:], d["gate"].rearrange("(k p) e -> p k e", p=P)).then_inc(gate_in, 16)

            def body(J):
                if seq_exists(J, 0):
                    need(sp, clo_done, J)
                    for i in range(2):
                        sp.dma_start(cT_raw[:, :, i], d["ctxT"][J * 2 + i].rearrange("(k p) s -> p k s", p=P)).then_inc(c_in, 16)
                for i in range(2):
                    if seq_exists(J, i):
                        need(sp, x_tr, upto_seq(J, i - 2))
                        sp.dma_start(x_raw[:, i], d["x1"][J * 2 + i].rearrange("(t p) c -> p t c", p=P)).then_inc(x_in[i], 16)
                    if seq_exists(J, i - 2):
                        need(sp, o_read, upto_seq(J, i - 3))
                        sp.dma_start(x_res[:], d["x1"][J * 2 + (i - 2)].rearrange("(t p) c -> p t c", p=P)).then_inc(res_in, 16)
                    if seq_exists(J, i - 3):
                        k = (i - 3) % 2
                        need(sp, x2_done, upto_seq(J, i - 3))
                        sp.dma_start(d["x2"][J * 2 + (i - 3)].rearrange("(t p) c -> p t c", p=P), x2[:, k]).then_inc(x2_out[k], 16)

            over_bodies(sp, body, 2, BODIES, BODIES + 2)
            for i in range(2):
                sp.wait_ge(x2_out[i], 16 * BODIES)

        @block.gpsimd
        def _(pool):
            pool.memset(half[:], -0.5).then_inc(const, 1)
            zeros = [k_hi[0:DH, :, :, S:2 * S], k_lo[0:DH, :, :, S:2 * S], k_hi[DH:P, :, :, 0:S], k_lo[DH:P, :, :, 0:S],
                     v_hi[:, :, :, DH:2 * DH], v_lo[:, :, :, DH:2 * DH]]
            pool.wait_ge(w_lo, len(names))
            for n, t in enumerate(zeros):
                pool.wait_ge(const, n + 1)
                pool.memset(f32(t), 0.0).then_inc(const, 1)
            pool.wait_ge(const, 7)

            def body(J):
                for m in range(BODY):
                    g = m - IL
                    if step_exists(J, g):
                        r = g % RING
                        need_alone(pool, inv_done, upto(J, g), spare_pool)
                        for t in range(TT):
                            for hh in range(2):
                                n = 2 * t + hh
                                ins = pool.tensor_scalar(prob[:, r, t, hh], prob[:, r, t, hh], inverse[:, r, n:n + 1], 1.0,
                                                         ALU.mult, ALU.mult)
                        ins.then_inc(p_done, 1)
                    if m % NP == NORM % NP and seq_exists(J, (m - NORM) // NP):
                        need(pool, ve_done, upto_seq(J, (m - NORM) // NP))
                        pool.tensor_tensor(rstd[:], var_eps[:], half[:], ALU.pow).then_inc(rstd_done, 1)

            over_bodies(pool, body, 1, BODIES, BODIES + 1)

        @block.tensor
        def _(pe):
            first_use = {1: (w_lo, 1), QL: (w_lo, 3), SL: (const, 7), OL: (w_lo, 5)}

            def body(J):
                for m in range(BODY):
                    if isinstance(J, int) and J == 0 and m in first_use:
                        pe.wait_ge(*first_use[m])
                    if m % NP == 0 and seq_exists(J, m // NP):
                        b = m // NP
                        need(pe, x_in[b], J * 16 + 16)
                        need(pe, x2Tlo_done, upto_seq(J, b - 3))
                        need(pe, xTlo_done, upto_seq(J, b - 1))
                        for k in range(KC):
                            for t in range(TT):
                                mm = pe.transpose(XT[:, k * T + t * P:k * T + t * P + P], x_raw[:, b, t, k * P:k * P + P], ident[:])
                        mm.then_inc(x_tr, 1)
                    if m % NP in (1, 2) and seq_exists(J, m // NP):
                        b, n = m // NP, m % NP - 1
                        need(pe, clo_done, J + 1)
                        need(pe, vlo_done, upto_seq(J, b, 2, n - 2))
                        need(pe, g_done, upto_seq(J, b - 3))
                        for k in range(KC):
                            half_n = slice(n * 512, n * 512 + 512)
                            mm = three(pe, M[0:S, :], cT_hi[:, k, b], cT_lo[:, k, b], w["wv"][0][:, k, half_n],
                                       w["wv"][1][:, k, half_n], k == 0, k == KC - 1)
                        mm.then_inc(v_mm, 1)
                    g = m - SL
                    if step_exists(J, g):
                        r, b, p = g % RING, (g // NP) % 2, g % NP
                        need(pe, qlo_done, upto(J, g))
                        if b == 0:
                            need(pe, klo_done, J * NP + p + 1 if g >= 0 else J * NP + p + 1 - NP)
                        need(pe, exp_done, upto(J, g - 2, 4))
                        for t in range(TT):
                            tk = slice(t * P, t * P + P)
                            mm = three(pe, SC[g % 2][:, t * 2 * S:(t + 1) * 2 * S], q_hi[:, r, tk], q_lo[:, r, tk], k_hi[:, b, p],
                                       k_lo[:, b, p], True, True)
                        mm.then_inc(s_mm, 1)
                    g = m - QL
                    if step_exists(J, g):
                        b, p = (g // NP) % 2, g % NP
                        if p == 0:
                            need(pe, xTlo_done, upto_seq(J, g // NP))
                        need(pe, qlo_done, upto(J, g - 1))
                        ws = slice(p * P, p * P + P)
                        if b == 1 and p == 0 and g >= 0:
                            need(pe, klo_done, J * NP + NP)
                        if b == 0:
                            jk = J * NP + p + 1
                            need(pe, clo_done, J + 1)
                            need(pe, klo_done, jk - 1)
                            for k in range(KC):
                                mm = three(pe, K, w["wk"][0][:, k, ws], w["wk"][1][:, k, ws],
                                           cT_hi[:, k].rearrange("p b s -> p (b s)"), cT_lo[:, k].rearrange("p b s -> p (b s)"),
                                           k == 0, k == KC - 1)
                            mm.then_inc(k_mm, 1)
                        for k in range(KC):
                            mm = three(pe, Q, w["wq"][0][:, k, ws], w["wq"][1][:, k, ws], xT_hi[:, b, k], xT_lo[:, b, k],
                                       k == 0, k == KC - 1)
                        mm.then_inc(q_mm, 1)
                    g = m - CL
                    if step_exists(J, g):
                        r, b, p = g % RING, (g // NP) % 2, g % NP
                        if p == 0:
                            need(pe, vlo_done, upto_seq(J, g // NP, 2))
                        need(pe, pTlo_done, upto(J, g))
                        need(pe, cxlo_done, upto(J, g - 1))
                        for hh in range(2):
                            win = slice(hh * DH, hh * DH + 2 * DH)
                            mm = three(pe, CX[:, 0:T], v_hi[:, b, p, win], v_lo[:, b, p, win], pT_hi[:, r, hh], pT_lo[:, r, hh],
                                       hh == 0, hh == 1)
                        mm.then_inc(cx_mm, 1)
                    g = m - TL
                    if step_exists(J, g):
                        r = g % RING
                        need(pe, p_done, upto(J, g))
                        need(pe, pTlo_done, upto(J, g - 1))
                        for hh in range(2):
                            for t in range(TT):
                                mm = pe.transpose(TR[0:S, hh * T + t * P:hh * T + t * P + P], prob[:, r, t, hh], ident[:])
                        mm.then_inc(p_tr, 1)
                    if m % NP == X2T % NP and seq_exists(J, (m - X2T) // NP):
                        b = (m - X2T) // NP
                        need(pe, x2_done, upto_seq(J, b))
                        need(pe, xTlo_done, at_most(upto_seq(J, b + 2), B))
                        for k in range(KC):
                            for t in range(TT):
                                mm = pe.transpose(XT[:, k * T + t * P:k * T + t * P + P], x2[:, b % 2, t, k * P:k * P + P], ident[:])
                        mm.then_inc(x2_tr, 1)
                    if m % NP == GATE % NP and seq_exists(J, (m - GATE) // NP):
                        b = (m - GATE) // NP
                        need(pe, x2Tlo_done, upto_seq(J, b))
                        need(pe, vlo_done, at_most(upto_seq(J, b + 2, 2), 2 * B))
                        for t in range(TT):
                            tk = slice(t * P, t * P + P)
                            for k in range(KC):
                                mm = three(pe, M[:, t * E:t * E + E], x2T_hi[:, k, tk], x2T_lo[:, k, tk], gate_hi[:, k],
                                           gate_lo[:, k], k == 0, k == KC - 1)
                        mm.then_inc(g_mm, 1)
                    g = m - OL
                    if step_exists(J, g):
                        r, p = g % RING, g % NP
                        need(pe, cxlo_done, upto(J, g))
                        if p == 0:
                            need(pe, o_read, upto_seq(J, g // NP - 1))
                        for t in range(TT):
                            tk = slice(t * P, t * P + P)
                            mm = three(pe, O[:, t * C:t * C + C], c_hi[:, r, tk], c_lo[:, r, tk], w["wo"][0][:, p], w["wo"][1][:, p],
                                       p == 0 and t == 0, p == NP - 1)
                        mm.then_inc(o_mm, 1)

            over_bodies(pe, body, 1, BODIES, BODIES + 1)

        @block.scalar
        def _(act):
            for n, name in enumerate(names):
                act.wait_ge(w_in[n], 16)
                act.activation(w[name][0][:].rearrange("p k n -> p (k n)"), raw[:, n], ACT.Copy, scale=CROSS_SCALE if name == "wq" else 1.0).then_inc(w_hi, 1)
            act.wait_ge(gate_in, 16)
            act.activation(gate_hi[:], gate_raw[:], ACT.Copy).then_inc(w_hi, 1)

            def body(J):
                for m in range(BODY):
                    if m == 0 and seq_exists(J, 0):
                        need(act, c_in, J * 32 + 32)
                        need(act, v_mm, J * 4)
                        need(act, k_mm, J * NP)
                        act.activation(cT_hi[:], cT_raw[:], ACT.Copy).then_inc(chi_done, 1)
                    if m % NP == 0 and seq_exists(J, m // NP):
                        b = m // NP
                        need(act, x_tr, upto_seq(J, b))
                        need(act, q_mm, upto(J, (b - 1) * NP - 1))
                        act.activation(xT_hi[:, b].rearrange("p k t -> p (k t)"), XT[:], ACT.Copy).then_inc(xThi_done, 1)
                    if m % NP in (1, 2) and seq_exists(J, m // NP):
                        b, n = m // NP, m % NP - 1
                        need(act, v_mm, upto_seq(J, b, 2, n - 1))
                        if n == 0:
                            need(act, cx_mm, upto(J, (b - 1) * NP - 1))
                        for hh in range(2):
                            ins = act.activation(v_hi[:, b, n * NP // 2:(n + 1) * NP // 2, hh * 2 * DH:hh * 2 * DH + DH],
                                                 M[0:S, :].rearrange("s (p h k) -> s p h k", h=2, k=DH)[:, :, hh], ACT.Copy)
                        ins.then_inc(vhi_done, 1)
                    g = m - QL
                    if step_exists(J, g):
                        r, b, p = g % RING, (g // NP) % 2, g % NP
                        need(act, q_mm, upto(J, g))
                        need(act, s_mm, upto(J, g - RING))
                        act.activation(q_hi[:, r], Q, ACT.Copy).then_inc(qhi_done, 1)
                        if b == 0:
                            jk = J * NP + p + 1
                            need(act, k_mm, jk)
                            need(act, s_mm, upto(J, g - NP))
                            for hh in range(2):
                                rows = slice(hh * DH, hh * DH + DH)
                                ins = act.activation(k_hi[rows, :, p, hh * S:hh * S + S],
                                                     QK[rows, T:T + 2 * S].rearrange("k (b s) -> k b s", b=2), ACT.Copy)
                            ins.then_inc(khi_done, 1)
                    g = m - CL
                    if step_exists(J, g):
                        r = g % RING
                        need(act, cx_mm, upto(J, g))
                        need(act, o_mm, upto(J, g - RING))
                        act.activation(c_hi[:, r], CX[:, 0:T], ACT.Copy).then_inc(cxhi_done, 1)
                    g = m - TL
                    if step_exists(J, g):
                        r = g % RING
                        need(act, p_tr, upto(J, g))
                        need(act, cx_mm, upto(J, g - RING))
                        act.activation(pT_hi[:, r].rearrange("s h t -> s (h t)"), TR[0:S, :], ACT.Copy).then_inc(pThi_done, 1)
                    if m % NP == X2T % NP and seq_exists(J, (m - X2T) // NP):
                        b = (m - X2T) // NP
                        need(act, x2_tr, upto_seq(J, b))
                        need(act, g_mm, upto_seq(J, b - 1))
                        act.activation(x2T_hi[:].rearrange("p k t -> p (k t)"), XT[:], ACT.Copy).then_inc(x2Thi_done, 1)
                    if m % NP == GATE % NP and seq_exists(J, (m - GATE) // NP):
                        b = (m - GATE) // NP
                        need_alone(act, g_mm, upto_seq(J, b), spare_act)
                        act.activation(logits[:, J * 2 + b].rearrange("p t e -> p (t e)"), M[:, 0:TT * E], ACT.Copy).then_inc(g_done, 1)
                    g = m - SL
                    if step_exists(J, g):
                        r = g % RING
                        need(act, max_done, upto(J, g))
                        need(act, p_tr, upto(J, g - RING))
                        for t in range(TT):
                            for hh in range(2):
                                n = 2 * t + hh
                                act.activation(prob[:, r, t, hh], SC[g % 2][:, n * S:n * S + S], ACT.Exp, bias=shift[:, r, n:n + 1],
                                               accum_out=total[:, r, n:n + 1]).then_inc(exp_done, 1)

            over_bodies(act, body, 1, BODIES, BODIES + 1)

        @block.vector
        def _(dve):
            for n, name in enumerate(names):
                dve.wait_ge(w_hi, n + 1)
                hi, lo = (t[:].rearrange("p k n -> p (k n)") for t in w[name])
                dve.scalar_tensor_tensor(out=lo, in0=raw[:, n], scalar=CROSS_SCALE if name == "wq" else 1.0, in1=f32(hi),
                                         op0=ALU.mult, op1=ALU.subtract).then_inc(w_lo, 1)
            dve.wait_ge(w_hi, 5)
            dve.tensor_tensor(gate_lo[:], gate_raw[:], f32(gate_hi[:]), ALU.subtract).then_inc(w_lo, 1)

            def body(J):
                for m in range(BODY):
                    if m == 0 and seq_exists(J, 0):
                        need(dve, chi_done, J + 1)
                        dve.tensor_tensor(cT_lo[:], cT_raw[:], f32(cT_hi[:]), ALU.subtract).then_inc(clo_done, 1)
                    if m % NP == 0 and seq_exists(J, m // NP):
                        b = m // NP
                        need(dve, xThi_done, upto_seq(J, b))
                        dve.tensor_tensor(xT_lo[:, b].rearrange("p k t -> p (k t)"), XT[:],
                                          f32(xT_hi[:, b].rearrange("p k t -> p (k t)")), ALU.subtract).then_inc(xTlo_done, 1)
                    if m % NP in (1, 2) and seq_exists(J, m // NP):
                        b, n = m // NP, m % NP - 1
                        need(dve, vhi_done, upto_seq(J, b, 2, n - 1))
                        for hh in range(2):
                            at = (slice(None), b, slice(n * NP // 2, (n + 1) * NP // 2), slice(hh * 2 * DH, hh * 2 * DH + DH))
                            ins = dve.tensor_tensor(v_lo[at], M[0:S, :].rearrange("s (p h k) -> s p h k", h=2, k=DH)[:, :, hh],
                                                    f32(v_hi[at]), ALU.subtract)
                        ins.then_inc(vlo_done, 1)
                    if m % NP == NORM % NP and seq_exists(J, (m - NORM) // NP):
                        b = (m - NORM) // NP
                        need(dve, o_mm, upto(J, (b + 1) * NP - 1))
                        need(dve, res_in, J * 32 + 16 * (b + 1))
                        dve.tensor_tensor(res[:].rearrange("p t c -> p (t c)"), O[:, 0:TT * C],
                                          x_res[:].rearrange("p t c -> p (t c)"), ALU.add).then_inc(o_read, 1)
                    g = m - SL
                    if step_exists(J, g):
                        r = g % RING
                        need(dve, s_mm, upto(J, g))
                        dve.tensor_reduce(shift[:, r], SC[g % 2][:, 0:TT * 2 * S].rearrange("p (n s) -> p n s", s=S), AXIS.X, ALU.max,
                                          negate=True).then_inc(max_done, 1)
                    g = m - IL
                    if step_exists(J, g):
                        r = g % RING
                        need(dve, exp_done, upto(J, g, 4))
                        dve.reciprocal(inverse[:, r], total[:, r]).then_inc(inv_done, 1)
                    g = m - QL
                    if step_exists(J, g):
                        r, b, p = g % RING, (g // NP) % 2, g % NP
                        need(dve, qhi_done, upto(J, g))
                        if b == 0:
                            need(dve, khi_done, J * NP + p + 1)
                        dve.tensor_tensor(q_lo[:, r], Q, f32(q_hi[:, r]), ALU.subtract).then_inc(qlo_done, 1)
                        if b == 0:
                            jk = J * NP + p + 1
                            for hh in range(2):
                                at = (slice(hh * DH, hh * DH + DH), slice(None), p, slice(hh * S, hh * S + S))
                                ins = dve.tensor_tensor(k_lo[at], QK[hh * DH:hh * DH + DH, T:T + 2 * S].rearrange("k (b s) -> k b s", b=2),
                                                        f32(k_hi[at]), ALU.subtract)
                            ins.then_inc(klo_done, 1)
                    g = m - CL
                    if step_exists(J, g):
                        r = g % RING
                        need(dve, cxhi_done, upto(J, g))
                        dve.tensor_tensor(c_lo[:, r], CX[:, 0:T], f32(c_hi[:, r]), ALU.subtract).then_inc(cxlo_done, 1)
                    g = m - TL
                    if step_exists(J, g):
                        r = g % RING
                        need(dve, pThi_done, upto(J, g))
                        dve.tensor_tensor(pT_lo[:, r].rearrange("s h t -> s (h t)"), TR[0:S, :],
                                          f32(pT_hi[:, r].rearrange("s h t -> s (h t)")), ALU.subtract).then_inc(pTlo_done, 1)
                    if m % NP == (NORM + 1) % NP and seq_exists(J, (m - NORM - 1) // NP):
                        b = (m - NORM - 1) // NP
                        need(dve, rstd_done, upto_seq(J, b))
                        need(dve, x2_out[b % 2], J * 16 + 16 * (b // 2))
                        for t in range(TT):
                            ins = dve.tensor_scalar(x2[:, b % 2, t], res[:, t], meanvar[:, t, 0:1], rstd[:, t:t + 1],
                                                    ALU.subtract, ALU.mult)
                        ins.then_inc(x2_done, 1)
                    if m % NP == NORM % NP and seq_exists(J, (m - NORM) // NP):
                        b = (m - NORM) // NP
                        need(dve, o_read, upto_seq(J, b))
                        for t in range(TT):
                            dve.bn_stats(stats[:, t], res[:, t]).then_inc(st_done, 1)
                        need_alone(dve, st_done, upto_seq(J, b, TT), spare_dve)
                        for t in range(TT):
                            dve.bn_aggr(meanvar[:, t], stats[:, t]).then_inc(mv_done, 1)
                        need(dve, mv_done, upto_seq(J, b, TT))
                        dve.tensor_scalar(var_eps[:], meanvar[:, :, 1], EPS, None, ALU.add).then_inc(ve_done, 1)
                    if m % NP == X2T % NP and seq_exists(J, (m - X2T) // NP):
                        b = (m - X2T) // NP
                        need(dve, x2Thi_done, upto_seq(J, b))
                        dve.tensor_tensor(x2T_lo[:].rearrange("p k t -> p (k t)"), XT[:],
                                          f32(x2T_hi[:].rearrange("p k t -> p (k t)")), ALU.subtract).then_inc(x2Tlo_done, 1)

            over_bodies(dve, body, 1, BODIES, BODIES + 1)




def route(nc, bank, ident, logits, index_col, weight_col, d):
    with ExitStack() as ctx:
        al = Alloc(nc, ctx, "rt")
        n_rows = B * TT
        best, total, inverse = al.sb("best", [P, n_rows]), al.sb("total", [P, n_rows]), al.sb("inverse", [P, n_rows])
        ex = al.sb("ex", [P, n_rows, E])
        score = al.sb("score", [P, TT, B * E])
        left = al.sb("left", [P, NG, T])
        value, index = al.sb("value", [P, NG, CAP]), al.sb("index", [P, NG, CAP], U32)
        index_f, index_b = al.sb("index_f", [P, NG, CAP]), al.sb("index_b", [P, NG, CAP], BF16)
        rows = al.sb("rows", [P, 2, P])

        soft, exp_done = al.sem("soft"), al.sem("exp_done")
        s_tr, left_done = al.sem("s_tr"), al.sem("left_done")
        top, found, as_float = al.sem("top"), al.sem("found"), al.sem("as_float")
        stored, rows_in, r_tr, col_done = al.sem("stored"), al.sem("rows_in"), al.sem("r_tr"), al.sem("col_done")

        block = ctx.enter_context(nc.Block())

        def bc(ap):
            return ap.rearrange("p (n o) -> p n o", o=1).broadcast_to([P, ap.shape[1], E])

        @block.sync
        def _(sp):
            by_row = "(g p) c -> p g c"
            sp.wait_ge(as_float, 2)
            sp.dma_start(d["index"].rearrange("b (e c) -> (b e) c", e=E).rearrange(by_row, p=P), index_f[:]).then_inc(stored, 16)
            sp.dma_start(d["index_b"].rearrange("b (e c) -> (b e) c", e=E).rearrange(by_row, p=P), index_b[:]).then_inc(stored, 16)
            sp.dma_start(d["value"].rearrange("b (e c) -> (b e) c", e=E).rearrange(by_row, p=P), value[:]).then_inc(stored, 16)
            sp.wait_ge(stored, 48)
            sp.dma_start(rows[:, 0], d["index"].rearrange("b (k m) -> (b k) m", m=P)).then_inc(rows_in, 16)
            sp.dma_start(rows[:, 1], d["value"].rearrange("b (k m) -> (b k) m", m=P)).then_inc(rows_in, 16)

        @block.scalar
        def _(act):
            act.wait_ge(soft, 2)
            act.activation(ex[:], ex[:], ACT.Exp).then_inc(exp_done, 1)

        @block.tensor
        def _(pe):
            pe.wait_ge(soft, 5)
            for g in range(NG):
                for t in range(TT):
                    at = (g % 2) * T + t * P
                    mm = pe.transpose(bank[g // 2][:, at:at + P], score[:, t, g * P:g * P + P], ident[:])
                if g % 2:
                    mm.then_inc(s_tr, 1)
            pe.wait_ge(rows_in, 32)
            for n in range(2):
                mm = pe.transpose(bank[2][:, n * P:n * P + P], rows[:, n], ident[:])
            mm.then_inc(r_tr, 1)

        @block.vector
        def _(dve):
            rows_of = logits[:].rearrange("p b t e -> p (b t) e")
            dve.tensor_reduce(best[:], rows_of, AXIS.X, ALU.max).then_inc(soft, 1)
            dve.wait_ge(soft, 1)
            dve.tensor_tensor(ex[:], rows_of, bc(best[:]), ALU.subtract).then_inc(soft, 1)
            dve.wait_ge(exp_done, 1)
            dve.tensor_reduce(total[:], ex[:], AXIS.X, ALU.add).then_inc(soft, 1)
            dve.wait_ge(soft, 3)
            dve.reciprocal(inverse[:], total[:]).then_inc(soft, 1)
            dve.wait_ge(soft, 4)
            for t in range(TT):
                ins = dve.tensor_tensor(score[:, t].rearrange("p (b e) -> p b e", e=E),
                                        ex[:].rearrange("p (b t) e -> p b t e", t=TT)[:, :, t],
                                        bc(inverse[:]).rearrange("p (b t) e -> p b t e", t=TT)[:, :, t], ALU.mult)
            ins.then_inc(soft, 1)
            for n in range(NG // 2):
                dve.wait_ge(s_tr, n + 1)
                dve.tensor_copy(left[:, 2 * n:2 * n + 2].rearrange("p g t -> p (g t)"), bank[n][:]).then_inc(left_done, 1)
            rounds = CAP // 8
            for r in range(rounds):
                at = slice(8 * r, 8 * r + 8)
                dve.wait_ge(left_done, 2 + NG * r)
                for g in range(NG):
                    dve.max(value[:, g, at], left[:, g]).then_inc(top, 1)
                dve.wait_ge(top, NG * (r + 1))
                for g in range(NG):
                    dve.max_index(index[:, g, at], value[:, g, at], left[:, g]).then_inc(found, 1)
                dve.wait_ge(found, NG * (r + 1))
                if r < rounds - 1:
                    for g in range(NG):
                        dve.match_replace(left[:, g], value[:, g, at], left[:, g], -1.0).then_inc(left_done, 1)
            dve.tensor_copy(index_f[:], index[:]).then_inc(as_float, 1)
            dve.tensor_copy(index_b[:], index[:]).then_inc(as_float, 1)
            dve.wait_ge(r_tr, 1)
            dve.tensor_copy(index_col[:].rearrange("p b k o -> p (b k o)"), bank[2][:, 0:P]).then_inc(col_done, 1)
            dve.tensor_copy(weight_col[:].rearrange("p b k o -> p (b k o)"), bank[2][:, P:2 * P]).then_inc(col_done, 1)



GATHER = 8
STAGED = 4


def gather(nc, bank, d):
    with ExitStack() as ctx:
        al = Alloc(nc, ctx, "ga")
        token = al.sb("token", [P, TT])
        x_raw = al.sb("x_raw", [P, 2, TT, C])
        x_hi, x_lo = al.split("x", [P, 2, TT, C])
        chosen = al.sb("chosen", [P, 2, E * CAP], BF16)
        onehot = al.sb("onehot", [P, 2, TT, E * CAP], F32R)
        out = al.sb("out", [P, 2, KC, E, STAGED, CAP])
        x_in = [al.sem(f"x_in{i}") for i in range(2)]
        c_in = [al.sem(f"c_in{i}") for i in range(2)]
        stored = [al.sem(f"stored{i}") for i in range(2)]
        const, xhi_done, xlo_done, hot_done = al.sem("const"), al.sem("xhi_done"), al.sem("xlo_done"), al.sem("hot_done")
        g_mm, act_out, dve_out = al.sem("g_mm"), al.sem("act_out"), al.sem("dve_out")
        last = B // GATHER

        def n_of(J, b, more=0):
            return J * GATHER + (b + 1 + more)

        def exists(J, b):
            return not isinstance(J, int) or 0 <= GATHER * J + b < B

        block = ctx.enter_context(nc.Block())

        @block.sync
        def _(sp):
            def body(J):
                for b in range(GATHER):
                    if exists(J, b):
                        i = b % 2
                        need(sp, xlo_done, n_of(J, b - 2))
                        sp.dma_start(x_raw[:, i], d["x2"][J * GATHER + b].rearrange("(t p) c -> p t c", p=P)).then_inc(x_in[i], 16)
                        need(sp, hot_done, n_of(J, b - 2))
                        sp.dma_start(chosen[:, i], d["index_b"][J * GATHER + b].rearrange("(o n) -> o n", o=1).broadcast_to([P, E * CAP])).then_inc(c_in[i], 16)

            over_bodies(sp, body, 1, last, last)

        @block.gpsimd
        def _(pool):
            pool.iota(token[:], pattern=[[P, TT]], base=0, channel_multiplier=1,
                      allow_small_or_imprecise_dtypes=True).then_inc(const, 1)

            def body(J):
                for b in range(-1, GATHER - 1):
                    if exists(J, b) and b % STAGED == STAGED - 1:
                        i = (b // STAGED) % 2
                        need_alone(pool, act_out, n_of(J, b), const)
                        need_alone(pool, dve_out, n_of(J, b), const)
                        cols = (J * (GATHER // STAGED) + b // STAGED)
                        for k in range(KC):
                            pool.dma_start(d["chosen"].rearrange("e (k p) (g n) -> k g p e n", p=P, n=STAGED * CAP)[k, cols],
                                           out[:, i, k].rearrange("p e s c -> p e (s c)")).then_inc(stored[i], 16)

            over_bodies(pool, body, 1, last, last + 1)
            for i in range(2):
                pool.wait_ge(stored[i], 16 * KC * B // (2 * STAGED))

        @block.tensor
        def _(pe):
            def body(J):
                for b in range(-1, GATHER - 1):
                    if exists(J, b):
                        i = b % 2
                        need(pe, xlo_done, n_of(J, b))
                        need(pe, hot_done, n_of(J, b))
                        need(pe, act_out, n_of(J, b - 2))
                        need(pe, dve_out, n_of(J, b - 2))
                        for k in range(KC):
                            ks = slice(k * P, k * P + P)
                            for t in range(TT):
                                pe.matmul(bank[2 * i + k][:], x_hi[:, i, t, ks], onehot[:, i, t], start=t == 0, stop=False)
                                mm = pe.matmul(bank[2 * i + k][:], x_lo[:, i, t, ks], onehot[:, i, t], start=False, stop=t == TT - 1)
                        mm.then_inc(g_mm, 1)

            over_bodies(pe, body, 1, last, last + 1)

        @block.scalar
        def _(act):
            def body(J):
                for b in range(GATHER):
                    if exists(J, b):
                        i = b % 2
                        need(act, x_in[i], J * (16 * GATHER // 2) + 16 * (b // 2 + 1))
                        need(act, g_mm, n_of(J, b - 2))
                        act.activation(x_hi[:, i], x_raw[:, i], ACT.Copy).then_inc(xhi_done, 1)
                    if exists(J, b - 1):
                        i, q = (b - 1) % 2, (b - 1) % STAGED
                        h = ((b - 1) // STAGED) % 2
                        need(act, g_mm, n_of(J, b - 1))
                        if q == 0:
                            need(act, stored[h], J * (16 * KC * GATHER // (2 * STAGED)) + (0 if b >= 0 else -16 * KC))
                        act.activation(out[:, h, 0, :, q], bank[2 * i][:].rearrange("p (e c) -> p e c", e=E), ACT.Copy).then_inc(act_out, 1)

            over_bodies(act, body, 1, last, last + 1)

        @block.vector
        def _(dve):
            dve.wait_ge(const, 1)

            def body(J):
                for b in range(GATHER):
                    if exists(J, b):
                        i = b % 2
                        need(dve, xhi_done, n_of(J, b))
                        dve.tensor_tensor(x_lo[:, i], x_raw[:, i], f32(x_hi[:, i]), ALU.subtract).then_inc(xlo_done, 1)
                        need(dve, c_in[i], J * (16 * GATHER // 2) + 16 * (b // 2 + 1))
                        for t in range(TT):
                            ins = dve.tensor_scalar(onehot[:, i, t], chosen[:, i], token[:, t:t + 1], None, ALU.is_equal)
                        ins.then_inc(hot_done, 1)
                    if exists(J, b - 1):
                        i, q = (b - 1) % 2, (b - 1) % STAGED
                        h = ((b - 1) // STAGED) % 2
                        need(dve, g_mm, n_of(J, b - 1))
                        if q == 0:
                            need(dve, stored[h], J * (16 * KC * GATHER // (2 * STAGED)) + (0 if b >= 0 else -16 * KC))
                        dve.tensor_copy(out[:, h, 1, :, q], bank[2 * i + 1][:].rearrange("p (e c) -> p e c", e=E)).then_inc(dve_out, 1)

            over_bodies(dve, body, 1, last, last + 1)


CHUNK = 512
CHUNKS = B * CAP // CHUNK
XBODY = 2 * CHUNKS
XBODIES = E // 2
WG, WU, WD = slice(0, KC * F), slice(KC * F, 2 * KC * F), slice(2 * KC * F, 2 * KC * F + FT * C)


def experts(nc, bank, d):
    with ExitStack() as ctx:
        al = Alloc(nc, ctx, "ex")
        n_w = 2 * KC * F + FT * C
        w_raw = al.sb("w_raw", [P, 2, n_w])
        w_hi, w_lo = al.split("w", [P, 2, n_w])
        x_raw = al.sb("x_raw", [P, 2, KC, CHUNK])
        x_hi, x_lo = al.split("x", [P, 2, KC, CHUNK])
        act_g = al.sb("act_g", [P, 2, CHUNK])
        hid = al.sb("hid", [P, 2, CHUNK])
        h_hi, h_lo = al.split("h", [P, 2, FT, CHUNK])
        out = al.sb("out", [P, 2, CHUNK // P, C])
        w_in = [al.sem(f"w_in{i}") for i in range(2)]
        x_in = [al.sem(f"x_in{i}") for i in range(2)]
        stored = [al.sem(f"stored{i}") for i in range(2)]
        whi_done, wlo_done, xhi_done, xlo_done = al.sem("whi_done"), al.sem("wlo_done"), al.sem("xhi_done"), al.sem("xlo_done")
        g_mm, u_mm, gelu_done, hid_done = al.sem("g_mm"), al.sem("u_mm"), al.sem("gelu_done"), al.sem("hid_done")
        hhi_done, hlo_done = al.sem("hhi_done"), al.sem("hlo_done")
        d_mm, act_out, dve_out = al.sem("d_mm"), al.sem("act_out"), al.sem("dve_out")
        GB, UB, DB = bank[0:2], bank[2:4], bank[4:8]

        def n_of(J, n, per=1, more=0):
            return J * (XBODY * per) + (per * (n + 1) + more)

        def exists(J, n):
            return not isinstance(J, int) or 0 <= XBODY * J + n < E * CHUNKS

        def weights(t, i, part, inner):
            return t[:, i, part].rearrange("p (k n) -> p k n", n=inner)

        GL, DL = 1, 2

        block = ctx.enter_context(nc.Block())

        @block.sync
        def _(sp):
            def body(J):
                for n in range(XBODY):
                    i, e = n % 2, n // CHUNKS
                    if exists(J, n):
                        if n % CHUNKS == 0:
                            need(sp, wlo_done, J * 2 + (e - 1))
                            for part, name, inner in ((WG, "eg", F), (WU, "eu", F), (WD, "ed", C)):
                                sp.dma_start(weights(w_raw, e, part, inner),
                                             d[name][J * 2 + e].rearrange("(k p) n -> p k n", p=P)).then_inc(w_in[e], 16)
                        need(sp, xlo_done, n_of(J, n - 2))
                        sp.dma_start(x_raw[:, i], d["chosen"][J * 2 + e].rearrange("(k p) n -> p k n", p=P)[
                            :, :, (n % CHUNKS) * CHUNK:(n % CHUNKS + 1) * CHUNK]).then_inc(x_in[i], 16)
                    m = n - DL - 1
                    if exists(J, m):
                        need(sp, act_out, n_of(J, m))
                        need(sp, dve_out, n_of(J, m))
                        rows = d["eo"][J * 2 + m // CHUNKS].rearrange("b c f -> (b c) f")
                        sp.dma_start(rows[(m % CHUNKS) * CHUNK:(m % CHUNKS + 1) * CHUNK].rearrange("(t p) f -> p t f", p=P),
                                     out[:, m % 2]).then_inc(stored[m % 2], 16)

            over_bodies(sp, body, 1, XBODIES, XBODIES + 1)
            for i in range(2):
                sp.wait_ge(stored[i], 16 * E * CHUNKS // 2)

        @block.tensor
        def _(pe):
            def body(J):
                for m in range(XBODY):
                    n = m - GL
                    if exists(J, n):
                        i, e = n % 2, (n // CHUNKS) % 2
                        need(pe, wlo_done, J * 2 + n // CHUNKS + 1)
                        need(pe, xlo_done, n_of(J, n))
                        wg, wu = [(weights(w_hi, e, part, F), weights(w_lo, e, part, F)) for part in (WG, WU)]
                        for f in range(FT):
                            fs = slice(f * P, f * P + P)
                            need(pe, gelu_done, n_of(J, n, FT, f - FT - 1))
                            for k in range(KC):
                                mm = three(pe, GB[f % 2][:], wg[0][:, k, fs], wg[1][:, k, fs], x_hi[:, i, k], x_lo[:, i, k],
                                           k == 0, k == KC - 1)
                            mm.then_inc(g_mm, 1)
                            need(pe, hid_done, n_of(J, n, FT, f - FT - 1))
                            for k in range(KC):
                                mm = three(pe, UB[f % 2][:], wu[0][:, k, fs], wu[1][:, k, fs], x_hi[:, i, k], x_lo[:, i, k],
                                           k == 0, k == KC - 1)
                            mm.then_inc(u_mm, 1)
                    n = m - DL
                    if exists(J, n):
                        i, e = n % 2, (n // CHUNKS) % 2
                        need(pe, hlo_done, n_of(J, n, FT))
                        need(pe, act_out, n_of(J, n - 2))
                        need(pe, dve_out, n_of(J, n - 2))
                        wd = weights(w_hi, e, WD, C), weights(w_lo, e, WD, C)
                        for t in range(CHUNK // P):
                            ts = slice(t * P, t * P + P)
                            to = DB[2 * i + t // 2][:, (t % 2) * C:(t % 2) * C + C]
                            for f in range(FT):
                                mm = three(pe, to, h_hi[:, i, f, ts], h_lo[:, i, f, ts], wd[0][:, f], wd[1][:, f], f == 0, f == FT - 1)
                            if t % 2:
                                mm.then_inc(d_mm, 1)

            over_bodies(pe, body, 1, XBODIES, XBODIES + 1)

        @block.scalar
        def _(act):
            def body(J):
                for m in range(XBODY):
                    n = m
                    if exists(J, n):
                        i, e = n % 2, n // CHUNKS
                        if n % CHUNKS == 0:
                            need(act, w_in[e], J * 48 + 48)
                            need(act, d_mm, n_of(J, (e - 1) * CHUNKS - 1, 2))
                            act.activation(w_hi[:, e], w_raw[:, e], ACT.Copy).then_inc(whi_done, 1)
                        need(act, x_in[i], J * (8 * XBODY) + 16 * (n // 2 + 1))
                        need(act, u_mm, n_of(J, n - 2, FT))
                        act.activation(x_hi[:, i], x_raw[:, i], ACT.Copy).then_inc(xhi_done, 1)
                    n = m - GL
                    if exists(J, n):
                        i = n % 2
                        need(act, d_mm, n_of(J, n - 2, 2))
                        for f in range(FT + 1):
                            if f < FT:
                                need(act, g_mm, n_of(J, n, FT, f - FT + 1))
                                need(act, hid_done, n_of(J, n, FT, f - FT - 1))
                                act.activation(act_g[:, f % 2], GB[f % 2][:], ACT.Gelu).then_inc(gelu_done, 1)
                            if f > 0:
                                need(act, hid_done, n_of(J, n, FT, f - FT))
                                act.activation(h_hi[:, i, f - 1], hid[:, (f - 1) % 2], ACT.Copy).then_inc(hhi_done, 1)
                    n = m - DL
                    if exists(J, n):
                        i = n % 2
                        need(act, d_mm, n_of(J, n, 2, -1))
                        need(act, stored[i], (J * (8 * XBODY) + 16 * (n // 2)))
                        act.activation(out[:, i, 0:2].rearrange("p t f -> p (t f)"), DB[2 * i][:], ACT.Copy).then_inc(act_out, 1)

            over_bodies(act, body, 1, XBODIES, XBODIES + 1)

        @block.vector
        def _(dve):
            def body(J):
                for m in range(XBODY):
                    n = m
                    if exists(J, n):
                        i, e = n % 2, n // CHUNKS
                        if n % CHUNKS == 0:
                            need(dve, whi_done, J * 2 + e + 1)
                            dve.tensor_tensor(w_lo[:, e], w_raw[:, e], f32(w_hi[:, e]), ALU.subtract).then_inc(wlo_done, 1)
                        need(dve, xhi_done, n_of(J, n))
                        dve.tensor_tensor(x_lo[:, i], x_raw[:, i], f32(x_hi[:, i]), ALU.subtract).then_inc(xlo_done, 1)
                    n = m - GL
                    if exists(J, n):
                        i = n % 2
                        for f in range(FT + 1):
                            if f < FT:
                                need(dve, u_mm, n_of(J, n, FT, f - FT + 1))
                                need(dve, gelu_done, n_of(J, n, FT, f - FT + 1))
                                need(dve, hhi_done, n_of(J, n, FT, f - FT - 1))
                                need(dve, hlo_done, n_of(J, n, FT, f - FT - 1))
                                dve.tensor_tensor(hid[:, f % 2], act_g[:, f % 2], UB[f % 2][:], ALU.mult).then_inc(hid_done, 1)
                            if f > 0:
                                need(dve, hhi_done, n_of(J, n, FT, f - FT))
                                dve.tensor_tensor(h_lo[:, i, f - 1], hid[:, (f - 1) % 2], f32(h_hi[:, i, f - 1]),
                                                  ALU.subtract).then_inc(hlo_done, 1)
                    n = m - DL
                    if exists(J, n):
                        i = n % 2
                        need(dve, d_mm, n_of(J, n, 2))
                        need(dve, stored[i], (J * (8 * XBODY) + 16 * (n // 2)))
                        dve.tensor_copy(out[:, i, 2:4].rearrange("p t f -> p (t f)"), DB[2 * i + 1][:]).then_inc(dve_out, 1)

            over_bodies(dve, body, 1, XBODIES, XBODIES + 1)




def combine(nc, bank, ident, index_col, weight_col, d):
    with ExitStack() as ctx:
        al = Alloc(nc, ctx, "co")
        names = ("sg", "su", "sd")
        w_raw = [al.sb(n + "_raw", [P, KC * F]) for n in names]
        wg, wu = al.split("sg", [P, KC, F]), al.split("su", [P, KC, F])
        wd = al.split("sd", [P, FT, C])
        token_row = al.sb("token_row", [P, T])
        half = al.sb("half", [P, TT])
        x_raw = al.sb("x_raw", [P, 2, TT, C])
        x_res = al.sb("x_res", [P, TT, C])
        xT_hi, xT_lo = al.split("xT", [P, 2, KC, T])
        eo_raw = al.sb("eo_raw", [P, 2, KS, C])
        eo_hi, eo_lo = al.split("eo", [P, 2, KS, C])
        onehot = al.sb("onehot", [P, 2, KS, T], F32R)
        act_g = al.sb("act_g", [P, 2, 2, T])
        hid = al.sb("hid", [P, 2, 2, T])
        h_hi, h_lo = al.split("h", [P, 2, FT, T])
        res = al.sb("res", [P, TT, C])
        stats, meanvar = al.sb("stats", [P, TT, 6]), al.sb("meanvar", [P, TT, 2])
        var_eps, rstd = al.sb("var_eps", [P, TT]), al.sb("rstd", [P, TT])
        y = al.sb("y", [P, 2, TT, C])
        XT, GB, UB, DB = bank[0], bank[1:3], bank[3:5], bank[5:7]

        w_in, w_hi, w_lo, const = al.sem("w_in"), al.sem("w_hi"), al.sem("w_lo"), al.sem("const")
        x_in = [al.sem(f"x_in{i}") for i in range(2)]
        eo_in = [al.sem(f"eo_in{i}") for i in range(2)]
        y_out = [al.sem(f"y_out{i}") for i in range(2)]
        res_in = al.sem("res_in")
        x_tr, xThi_done, xTlo_done = al.sem("x_tr"), al.sem("xThi_done"), al.sem("xTlo_done")
        eohi_done, eolo_done, hot_done = al.sem("eohi_done"), al.sem("eolo_done"), al.sem("hot_done")
        g_mm, u_mm, gelu_done, hid_done = al.sem("g_mm"), al.sem("u_mm"), al.sem("gelu_done"), al.sem("hid_done")
        hhi_done, hlo_done, d_mm, o_read = al.sem("hhi_done"), al.sem("hlo_done"), al.sem("d_mm"), al.sem("o_read")
        st_done, mv_done, ve_done, rstd_done, y_done = (
            al.sem("st_done"), al.sem("mv_done"), al.sem("ve_done"), al.sem("rstd_done"), al.sem("y_done"))
        spare_act, spare_dve = al.sem("spare_act"), al.sem("spare_dve")

        GL, DL, NL = 1, 2, 3
        FP = FT // 2

        block = ctx.enter_context(nc.Block())

        @block.sync
        def _(sp):
            for n, name in enumerate(names):
                sp.dma_start(w_raw[n][:].rearrange("p (k n) -> p k n", k=KC if name != "sd" else FT),
                             d[name].rearrange("(k p) n -> p k n", p=P)).then_inc(w_in, 16)

            def body(J):
                for i in range(2):
                    if seq_exists(J, i):
                        need(sp, x_tr, upto_seq(J, i - 2))
                        sp.dma_start(x_raw[:, i], d["x2"][J * 2 + i].rearrange("(t p) c -> p t c", p=P)).then_inc(x_in[i], 16)
                        need(sp, eolo_done, upto_seq(J, i - 2, KS))
                        for q in range(P // CAP):
                            sp.dma_start(eo_raw[q * CAP:(q + 1) * CAP, i],
                                         d["eo"].rearrange("(k q) b c f -> q b c k f", k=KS)[q, J * 2 + i]).then_inc(eo_in[i], 16)
                    if seq_exists(J, i - 2):
                        need(sp, o_read, upto_seq(J, i - 3))
                        sp.dma_start(x_res[:], d["x2"][J * 2 + (i - 2)].rearrange("(t p) c -> p t c", p=P)).then_inc(res_in, 16)
                    if seq_exists(J, i - 4):
                        k = i % 2
                        need(sp, y_done, upto_seq(J, i - 4))
                        sp.dma_start(d["out"][J * 2 + (i - 4)].rearrange("(t p) c -> p t c", p=P), y[:, k]).then_inc(y_out[k], 16)

            over_bodies(sp, body, 2, BODIES, BODIES + 2)
            for i in range(2):
                sp.wait_ge(y_out[i], 16 * BODIES)

        @block.gpsimd
        def _(pool):
            pool.iota(token_row[:], pattern=[[1, T]], base=0, channel_multiplier=0,
                      allow_small_or_imprecise_dtypes=True).then_inc(const, 1)
            pool.memset(half[:], -0.5).then_inc(const, 1)
            pool.wait_ge(const, 2)

            def body(J):
                for m in range(2):
                    if seq_exists(J, m - NL):
                        need(pool, ve_done, upto_seq(J, m - NL))
                        pool.tensor_tensor(rstd[:], var_eps[:], half[:], ALU.pow).then_inc(rstd_done, 1)

            over_bodies(pool, body, 2, BODIES, BODIES + 2)

        @block.tensor
        def _(pe):
            pe.wait_ge(w_lo, 3)

            def body(J):
                for m in range(2):
                    if seq_exists(J, m):
                        need(pe, x_in[m], J * 16 + 16)
                        need(pe, xTlo_done, upto_seq(J, m - 1))
                        for k in range(KC):
                            for t in range(TT):
                                mm = pe.transpose(XT[:, k * T + t * P:k * T + t * P + P], x_raw[:, m, t, k * P:k * P + P], ident[:])
                        mm.then_inc(x_tr, 1)
                    b = m - GL
                    if seq_exists(J, b):
                        i = b % 2
                        need(pe, xTlo_done, upto_seq(J, b))
                        for fp in range(FP):
                            for to, w, read, mmd in ((GB[fp], wg, gelu_done, g_mm), (UB[fp], wu, hid_done, u_mm)):
                                need(pe, read, upto_seq(J, b - 1, FP, fp - FP + 1))
                                for f in range(2):
                                    fs = slice((2 * fp + f) * P, (2 * fp + f + 1) * P)
                                    for k in range(KC):
                                        mm = three(pe, to[:, f * T:f * T + T], w[0][:, k, fs], w[1][:, k, fs], xT_hi[:, i, k],
                                                   xT_lo[:, i, k], k == 0, k == KC - 1)
                                mm.then_inc(mmd, 1)
                    b = m - DL
                    if seq_exists(J, b):
                        i = b % 2
                        need(pe, hlo_done, upto_seq(J, b, FP))
                        need(pe, hot_done, upto_seq(J, b))
                        need(pe, eolo_done, upto_seq(J, b, KS))
                        need(pe, o_read, upto_seq(J, b - 2))
                        for t in range(TT):
                            ts = slice(t * P, t * P + P)
                            to = DB[i][:, t * C:t * C + C]
                            for f in range(FT):
                                three(pe, to, h_hi[:, i, f, ts], h_lo[:, i, f, ts], wd[0][:, f], wd[1][:, f], f == 0, False)
                            for k in range(KS):
                                pe.matmul(to, onehot[:, i, k, ts], eo_hi[:, i, k], start=False, stop=False, skip_group_check=True)
                                mm = pe.matmul(to, onehot[:, i, k, ts], eo_lo[:, i, k], start=False, stop=k == KS - 1,
                                               skip_group_check=True)
                        mm.then_inc(d_mm, 1)

            over_bodies(pe, body, 2, BODIES, BODIES + 2)

        @block.scalar
        def _(act):
            act.wait_ge(w_in, 48)
            for n, w in enumerate((wg, wu, wd)):
                act.activation(w[0][:].rearrange("p k n -> p (k n)"), w_raw[n][:], ACT.Copy).then_inc(w_hi, 1)

            def body(J):
                for m in range(2):
                    if seq_exists(J, m):
                        need(act, x_tr, upto_seq(J, m))
                        need(act, u_mm, upto_seq(J, m - 2, FP))
                        act.activation(xT_hi[:, m].rearrange("p k t -> p (k t)"), XT[:], ACT.Copy).then_inc(xThi_done, 1)
                    b = m - GL
                    if seq_exists(J, b):
                        i = b % 2
                        for fp in range(FP):
                            need(act, g_mm, upto_seq(J, b, FP, fp - FP + 1))
                            need(act, hid_done, upto_seq(J, b - 1, FP, fp - FP + 1))
                            act.activation(act_g[:, fp].rearrange("p f t -> p (f t)"), GB[fp][:], ACT.Gelu).then_inc(gelu_done, 1)
                        need(act, eo_in[i], J * 64 + 64 * (b // 2 + 1))
                        need_alone(act, d_mm, upto_seq(J, b - 2), spare_act)
                        for k in range(KS):
                            act.activation(eo_hi[:, i, k], eo_raw[:, i, k], ACT.Copy,
                                           scale=weight_col[:, J * 2 + b, k]).then_inc(eohi_done, 1)
                        for fp in range(FP):
                            need(act, hid_done, upto_seq(J, b, FP, fp - FP + 1))
                            act.activation(h_hi[:, i, 2 * fp:2 * fp + 2], hid[:, fp], ACT.Copy).then_inc(hhi_done, 1)

            over_bodies(act, body, 2, BODIES, BODIES + 2)

        @block.vector
        def _(dve):
            for n, w in enumerate((wg, wu, wd)):
                dve.wait_ge(w_hi, n + 1)
                dve.tensor_tensor(w[1][:].rearrange("p k n -> p (k n)"), w_raw[n][:], f32(w[0][:].rearrange("p k n -> p (k n)")),
                                  ALU.subtract).then_inc(w_lo, 1)
            dve.wait_ge(const, 2)

            def body(J):
                for m in range(2):
                    if seq_exists(J, m):
                        need(dve, xThi_done, upto_seq(J, m))
                        dve.tensor_tensor(xT_lo[:, m].rearrange("p k t -> p (k t)"), XT[:],
                                          f32(xT_hi[:, m].rearrange("p k t -> p (k t)")), ALU.subtract).then_inc(xTlo_done, 1)
                    b = m - NL
                    if seq_exists(J, b):
                        need(dve, d_mm, upto_seq(J, b))
                        need(dve, res_in, J * 32 + 16 * (b + 1))
                        need(dve, y_done, upto_seq(J, b - 1))
                        dve.tensor_tensor(res[:].rearrange("p t c -> p (t c)"), DB[b % 2][:],
                                          x_res[:].rearrange("p t c -> p (t c)"), ALU.add).then_inc(o_read, 1)
                        need(dve, o_read, upto_seq(J, b))
                        for t in range(TT):
                            dve.bn_stats(stats[:, t], res[:, t]).then_inc(st_done, 1)
                        need_alone(dve, st_done, upto_seq(J, b, TT), spare_dve)
                        for t in range(TT):
                            dve.bn_aggr(meanvar[:, t], stats[:, t]).then_inc(mv_done, 1)
                        need(dve, mv_done, upto_seq(J, b, TT))
                        dve.tensor_scalar(var_eps[:], meanvar[:, :, 1], EPS, None, ALU.add).then_inc(ve_done, 1)
                    b = m - GL
                    if seq_exists(J, b):
                        i = b % 2
                        need(dve, d_mm, upto_seq(J, b - 2))
                        for k in range(KS):
                            ins = dve.tensor_scalar(onehot[:, i, k], token_row[:], index_col[:, J * 2 + b, k], None, ALU.is_equal)
                        ins.then_inc(hot_done, 1)
                        for fp in range(FP):
                            need(dve, u_mm, upto_seq(J, b, FP, fp - FP + 1))
                            need(dve, gelu_done, upto_seq(J, b, FP, fp - FP + 1))
                            need(dve, hhi_done, upto_seq(J, b - 1, FP, fp - FP + 1))
                            need(dve, hlo_done, upto_seq(J, b - 1, FP, fp - FP + 1))
                            dve.tensor_tensor(hid[:, fp].rearrange("p f t -> p (f t)"), act_g[:, fp].rearrange("p f t -> p (f t)"),
                                              UB[fp][:], ALU.mult).then_inc(hid_done, 1)
                        for k in range(KS):
                            need(dve, eohi_done, upto_seq(J, b, KS, k - KS + 1))
                            dve.scalar_tensor_tensor(out=eo_lo[:, i, k], in0=eo_raw[:, i, k], scalar=weight_col[:, J * 2 + b, k],
                                                     in1=f32(eo_hi[:, i, k]), op0=ALU.mult, op1=ALU.subtract).then_inc(eolo_done, 1)
                        for fp in range(FP):
                            need(dve, hhi_done, upto_seq(J, b, FP, fp - FP + 1))
                            dve.tensor_tensor(h_lo[:, i, 2 * fp:2 * fp + 2], hid[:, fp], f32(h_hi[:, i, 2 * fp:2 * fp + 2]),
                                              ALU.subtract).then_inc(hlo_done, 1)
                    b = m - NL
                    if seq_exists(J, b):
                        need(dve, rstd_done, upto_seq(J, b))
                        need(dve, y_out[b % 2], J * 16 + 16 * (b // 2))
                        for t in range(TT):
                            ins = dve.tensor_scalar(y[:, b % 2, t], res[:, t], meanvar[:, t, 0:1], rstd[:, t:t + 1],
                                                    ALU.subtract, ALU.mult)
                        ins.then_inc(y_done, 1)

            over_bodies(dve, body, 2, BODIES, BODIES + 2)


def program(nc, d):
    with ExitStack() as ctx:
        al = Alloc(nc, ctx, "all")
        bank = [ctx.enter_context(nc.psum_tensor(f"bank{i}", [P, 512], F32)) for i in range(8)]
        ident = al.sb("ident", [P, P])
        logits = al.sb("logits", [P, B, TT, E])
        index_col = al.sb("index_col", [P, B, KS, 1])
        weight_col = al.sb("weight_col", [P, B, KS, 1])
        made = al.sem("made")
        with nc.Block() as block:
            @block.gpsimd
            def _(pool):
                pool.memset(ident[:], 0.0).then_inc(made, 1)
                pool.wait_ge(made, 1)
                pool.affine_select(out=ident[:], in_=ident[:], compare_op=ALU.not_equal, fill=1.0, base=0,
                                   pattern=[[-1, P]], channel_multiplier=1).then_inc(made, 1)
                pool.wait_ge(made, 2)
        self_attention(nc, bank, ident, d)
        cross_attention(nc, bank, ident, logits, d)
        route(nc, bank, ident, logits, index_col, weight_col, d)
        gather(nc, bank, d)
        experts(nc, bank, d)
        combine(nc, bank, ident, index_col, weight_col, d)




def kernel(**inputs):
    import concourse.bacc as bacc
    from concourse.bass_utils import run_bass_kernel_spmd

    def a(name):
        return np.asarray(inputs[name])

    def t(name):
        return np.swapaxes(a(name), -1, -2)

    def again(v, axis):
        return np.concatenate((v, np.take(v, range(REST, L), axis)), axis)

    ow = a("L0_attn_out_w").reshape(H, L, C).transpose(1, 0, 2).reshape(L, H * C)
    laid = {
        "x": a("x"), "xT": t("x"), "ctxT": t("ctx_1024"),
        "wd": again(a("L0_attn_Wd_w").transpose(1, 0, 2), 2).reshape(C, H * P),
        "lw": again(a("L0_attn_latent_w"), 1),
        "ow_a": again(ow, 0),
        "ow_b": np.concatenate((ow, np.zeros((AT - L, H * C), ow.dtype), ow[:REST], np.zeros((P - AT - REST, H * C), ow.dtype))),
        "qbias": again(t("L0_attn_Wd_b"), 0), "lbias": again(a("L0_attn_latent_b").reshape(L, 1), 0),
        "obias": np.broadcast_to(a("L0_attn_out_b"), (P, C)),
        "wq": a("L0_xattn_Wq").reshape(C, H * DH), "wk": a("L0_xattn_Wk").reshape(C, H * DH),
        "wv": a("L0_xattn_Wv").reshape(C, H * DH),
        "wo": a("L0_xattn_Wo").reshape(NP, P, C).transpose(1, 0, 2).reshape(P, NP * C),
        "gate": t("L0_ffn_gate_w"),
        "eg": t("L0_ffn_Wg"), "eu": t("L0_ffn_Wu"), "ed": t("L0_ffn_Wd"),
        "sg": t("L0_ffn_Ws_g"), "su": t("L0_ffn_Ws_u"), "sd": t("L0_ffn_Ws_d"),
    }
    nc = bacc.Bacc("TRN2", target_bir_lowering=False, num_devices=1)
    arrays, d = {}, {}
    for name, v in laid.items():
        arrays[f"in_{name}"] = np.ascontiguousarray(v)
        d[name] = nc.dram_tensor(f"in_{name}", v.shape, F32, kind="ExternalInput").ap()
    for name, shape, dt in (("x1", (B, T, C), F32), ("x2", (B, T, C), F32), ("index", (B, E * CAP), F32),
                            ("index_b", (B, E * CAP), BF16), ("value", (B, E * CAP), F32),
                            ("chosen", (E, C, B * CAP), F32), ("eo", (E, B, CAP, C), F32)):
        d[name] = nc.dram_tensor(f"mid_{name}", shape, dt, kind="Internal").ap()
    d["out"] = nc.dram_tensor("out", (B, T, C), F32, kind="ExternalOutput").ap()
    program(nc, d)
    return run_bass_kernel_spmd(nc, [arrays], core_ids=[0]).results[0]["out"]
```

```python
from contextlib import ExitStack

import numpy as np

import concourse.bass as bass
from concourse import mybir

F32 = mybir.dt.float32
F32R = mybir.dt.float32r
U32 = mybir.dt.uint32
ALU = mybir.AluOpType
ACT = mybir.ActivationFunctionType
AXIS = mybir.AxisListType

P = 128
B, T, C = 32, 256, 256
H, L = 16, 72
S, DH = 120, 64
E, F = 16, 512
CAP = int(T * 2.0 / E)
KC = C // P
TT = T // P
NP = H // 2
BODY = 2 * NP
BODIES = B // 2
RING = 4
FT = F // P
KS = E * CAP // P
GB = P // E
NG = B // GB
REST = 2 * L - P
AT = 96
GATHERS = B * CAP // P
Q4 = P // CAP
N_W = 2 * KC * F + F // P * C
WD_PARTS = 4
EPS = 1e-5
MASKED = -3e38
SELF_SCALE = float(C // H) ** -0.5
CROSS_SCALE = float(DH) ** -0.5


def need(eng, sem, count):
    if not isinstance(count, int) or count > 0:
        eng.wait_ge(sem, count)


def need_alone(eng, sem, count, spare):
    if not isinstance(count, int) or count > 0:
        eng.wait_ge(sem, count)
        eng.sem_inc(spare, 1)


def upto(J, g, per=1, more=0):
    return J * (BODY * per) + (per * (g + 1) + more)


def upto_seq(J, b, per=1, more=0):
    return J * (2 * per) + (per * (b + 1) + more)


def at_most(count, most):
    return min(count, most) if isinstance(count, int) else count


def step_exists(J, g):
    return not isinstance(J, int) or 0 <= BODY * J + g < B * NP


def seq_exists(J, b):
    return not isinstance(J, int) or 0 <= 2 * J + b < B


def over_bodies(eng, body, first, end, after):
    for J in range(first):
        body(J)
    with eng.Fori(first, end) as J:
        body(J)
    for J in range(end, after):
        body(J)


def three(pe, out, stat_hi, stat_lo, mov_hi, mov_lo, start, stop):
    pe.matmul(out, stat_hi, mov_hi, start=start, stop=False, skip_group_check=True)
    pe.matmul(out, stat_hi, mov_lo, start=False, stop=False, skip_group_check=True)
    return pe.matmul(out, stat_lo, mov_hi, start=False, stop=stop, skip_group_check=True)


def two(pe, out, stat_hi, stat_lo, mov_hi, mov_lo, start, stop):
    pe.matmul(out, stat_hi, mov_hi, start=start, stop=False, skip_group_check=True)
    rows = slice(0, AT + REST)
    return pe.matmul(out, stat_lo[rows], mov_lo[rows], start=False, stop=stop, skip_group_check=True)


class Alloc:

    def __init__(self, nc, ctx, tag):
        self.nc, self.ctx, self.tag, self.sems = nc, ctx, tag, []
        ctx.callback(self.clear)

    def sb(self, name, shape, dt=F32):
        return self.ctx.enter_context(self.nc.sbuf_tensor(f"{self.tag}_{name}", shape, dt))

    def split(self, name, shape):
        return self.sb(name + "_hi", shape, F32R), self.sb(name + "_lo", shape, F32R)

    def sem(self, name):
        self.sems.append(self.nc.alloc_semaphore(name=f"{self.tag}_{name}"))
        return self.sems[-1]

    def clear(self):
        self.nc.clear_and_free_semaphores(self.sems)
        self.nc.all_engine_barrier()


def f32(ap):
    return ap.bitcast(F32)




def self_attention(nc, bank, ident, wv_raw, wv_in, d):
    with ExitStack() as ctx:
        al = Alloc(nc, ctx, "sa")
        wd_hi, wd_lo = al.split("wd", [P, KC, H * P])
        lw_hi, lw_lo = al.split("lw", [P, KC, P])
        ow = al.sb("ow", [P, 2, H * C], F32R)
        qbias, lbias, obias = al.sb("qbias", [P, H]), al.sb("lbias", [P, 1]), al.sb("obias", [P, C])
        ones, minus_low = al.sb("ones", [P, 1]), al.sb("minus_low", [P, 1])
        mask = al.sb("mask", [P, 3, P])
        half = al.sb("half", [P, TT])
        xT_raw = al.sb("xT_raw", [P, 2, KC, T])
        x_hi, x_lo = al.split("xT", [P, 2, KC, T])
        x_res = al.sb("x_res", [P, 2, TT, C])
        kvT = al.sb("kvT", [P, T])
        kvT_a, kvT_b = al.sb("kvT_a", [P, 2, T], F32R), al.sb("kvT_b", [P, 2, T], F32R)
        kv_hi, kv_lo = al.split("kv", [P, 2, TT, P])
        q_hi, q_lo = al.split("q", [P, RING, 2, T])
        shift = al.sb("shift", [P, RING, 4])
        total = al.sb("total", [P, RING, 4])
        inverse = al.sb("inverse", [P, RING, 4])
        res = al.sb("res", [P, TT, C])
        stats, meanvar = al.sb("stats", [P, TT, 6]), al.sb("meanvar", [P, TT, 2])
        var_eps, rstd = al.sb("var_eps", [P, TT]), al.sb("rstd", [P, TT])
        x1 = al.sb("x1", [P, 2, TT, C])
        with ExitStack() as first:
            wd_raw = first.enter_context(nc.sbuf_tensor("sa_wd_raw", [P, KC, H * P], F32))
            lw_raw = first.enter_context(nc.sbuf_tensor("sa_lw_raw", [P, KC, P], F32))
            used = KC * (H + 1) * P
            first.enter_context(nc.sbuf_tensor("sa_between", [P, 3 * RING * 2 * 3 * P - used], F32))
            ow_raw = first.enter_context(nc.sbuf_tensor("sa_ow_raw", [P, 2, H * C], F32))
        prob = al.sb("prob", [P, RING, 2, 3 * P])
        pT_hi, pT_lo = al.split("pT", [P, RING, 2, 3 * P])
        y_hi, y_lo = al.split("y", [P, RING, 2, T])

        Q, SC, TR, PV, O, KV = bank[0], bank[1:3], bank[3:5], bank[5], bank[6], bank[7]

        lw_in, w_hi, w_lo, const = al.sem("lw_in"), al.sem("w_hi"), al.sem("w_lo"), al.sem("const")
        wd_in = [al.sem(f"wd_in{n}") for n in range(WD_PARTS)]
        ow_in, owhi_done, ow_done = al.sem("ow_in"), al.sem("owhi_done"), al.sem("ow_done")
        xT_in = [al.sem(f"xT_in{i}") for i in range(2)]
        res_in = [al.sem(f"res_in{i}") for i in range(2)]
        x1_out = [al.sem(f"x1_out{i}") for i in range(2)]
        xhi_done, xlo_done, xres_done = al.sem("xhi_done"), al.sem("xlo_done"), al.sem("xres_done")
        kvT_mm, kvT_done, kvTb_done = al.sem("kvT_mm"), al.sem("kvT_done"), al.sem("kvTb_done")
        kv_tr, kvhi_done, kv_done = al.sem("kv_tr"), al.sem("kvhi_done"), al.sem("kv_done")
        qdup_done, ydup_done = al.sem("qdup_done"), al.sem("ydup_done")
        q_mm, qhi_done, qlo_done = al.sem("q_mm"), al.sem("qhi_done"), al.sem("qlo_done")
        s_mm, s_read, exp_done = al.sem("s_mm"), al.sem("s_read"), al.sem("exp_done")
        inv_done, p_done = al.sem("inv_done"), al.sem("p_done")
        p_tr, pThi_done, pTlo_done = al.sem("p_tr"), al.sem("pThi_done"), al.sem("pTlo_done")
        pv_mm, yhi_done, ylo_done = al.sem("pv_mm"), al.sem("yhi_done"), al.sem("ylo_done")
        o_mm, o_read = al.sem("o_mm"), al.sem("o_read")
        st_done, mv_done, ve_done, rstd_done, x1_done = (
            al.sem("st_done"), al.sem("mv_done"), al.sem("ve_done"), al.sem("rstd_done"), al.sem("x1_done"))
        spare_dve, spare_pool = al.sem("spare_dve"), al.sem("spare_pool")

        def wd_part(n):
            return slice(n * H * P // WD_PARTS, (n + 1) * H * P // WD_PARTS)

        QL, SL, IL, TL, PL, OL = 1, 3, 4, 5, 7, 9
        KV_MM, KV_TR, RES, NORM = 2, 4, 12, 17

        OW_FROM, OW_PARTS = 3, 4
        OW_COLS = 2 * H * C // OW_PARTS
        ow_flat, ow_raw_flat = ow[:].rearrange("p a n -> p (a n)"), ow_raw[:].rearrange("p a n -> p (a n)")

        block = ctx.enter_context(nc.Block())

        @block.sync
        def _(sp):
            def load_wd(n):
                sp.dma_start(wd_raw[:, :, wd_part(n)], d["wd"].rearrange("(k p) n -> p k n", p=P)[:, :, wd_part(n)]).then_inc(wd_in[n], 16)

            sp.dma_start(lw_raw[:], d["lw"].rearrange("(k p) n -> p k n", p=P)).then_inc(lw_in, 16)
            sp.dma_start(qbias[:], d["qbias"]).then_inc(lw_in, 16)
            sp.dma_start(lbias[:], d["lbias"]).then_inc(lw_in, 16)

            def body(J):
                for i in range(2):
                    if seq_exists(J, i):
                        need(sp, xlo_done, upto_seq(J, i - 2))
                        sp.dma_start(xT_raw[:, i], d["xT"][J * 2 + i].rearrange("(k p) t -> p k t", p=P)).then_inc(xT_in[i], 16)
                        if isinstance(J, int) and J == 0:
                            for n in range(WD_PARTS)[slice(0, 2) if i == 0 else slice(2, None)]:
                                load_wd(n)
                        need(sp, o_read, upto_seq(J, i - 2))
                        sp.dma_start(x_res[:, i], d["x"][J * 2 + i].rearrange("(t p) c -> p t c", p=P)).then_inc(res_in[i], 16)
                    if isinstance(J, int) and J == 0 and i == 1:
                        sp.dma_start(ow_raw[:, 0], d["ow_a"]).then_inc(ow_in, 16)
                        sp.dma_start(ow_raw[:, 1], d["ow_b"]).then_inc(ow_in, 16)
                        sp.dma_start(obias[:], d["obias"]).then_inc(ow_in, 16)
                        sp.dma_start(wv_raw[:], d["wv"].rearrange("(k p) n -> p k n", p=P)).then_inc(wv_in, 16)
                    if seq_exists(J, i - 3):
                        k = (i - 3) % 2
                        need(sp, x1_done, upto_seq(J, i - 3))
                        sp.dma_start(d["x1"][J * 2 + (i - 3)].rearrange("(t p) c -> p t c", p=P), x1[:, k]).then_inc(x1_out[k], 16)

            over_bodies(sp, body, 2, BODIES, BODIES + 2)
            for i in range(2):
                sp.wait_ge(x1_out[i], 16 * BODIES)

        @block.gpsimd
        def _(pool):
            pool.memset(mask[:], 0.0).then_inc(const, 1)
            pool.memset(half[:], -0.5).then_inc(const, 1)
            pool.memset(minus_low[:], -1.0).then_inc(const, 1)
            pool.memset(f32(kvT_b[:]), 0.0).then_inc(const, 1)
            pool.wait_ge(const, 4)
            pool.affine_select(out=minus_low[:], in_=minus_low[:], compare_op=ALU.is_ge, fill=0.0, base=-L,
                               pattern=[[0, 1]], channel_multiplier=1).then_inc(const, 1)
            pool.affine_select(out=mask[:, 0], in_=mask[:, 0], compare_op=ALU.is_ge, fill=MASKED, base=0,
                               pattern=[[-1, P]], channel_multiplier=1).then_inc(const, 1)
            pool.affine_select(out=mask[:, 2], in_=mask[:, 2], compare_op=ALU.is_ge, fill=MASKED, base=0,
                               pattern=[[-1, P]], channel_multiplier=1).then_inc(const, 1)
            pool.wait_ge(const, 7)

            def body(J):
                for m in range(BODY):
                    if m % NP == RES % NP and seq_exists(J, (m - RES) // NP):
                        b = (m - RES) // NP
                        i = b % 2
                        if isinstance(J, int) and J == 0 and b == 0:
                            pool.wait_ge(ow_in, 48)
                        need(pool, res_in[i], J * 16 + 16 * (b // 2 + 1))
                        for t in range(TT):
                            pool.tensor_tensor(x_res[:, i, t], x_res[:, i, t], obias[:], ALU.add).then_inc(xres_done, 1)
                        need(pool, xres_done, upto_seq(J, b, TT))
                    g = m - IL
                    if step_exists(J, g):
                        r = g % RING
                        need_alone(pool, inv_done, upto(J, g), spare_pool)
                        for hh in range(2):
                            pool.tensor_scalar(prob[:, r, hh, 0:P], prob[:, r, hh, 0:P], inverse[:, r, 2 * hh:2 * hh + 1],
                                               1.0, ALU.mult, ALU.mult)
                            pool.tensor_scalar(prob[:, r, hh, P:3 * P], prob[:, r, hh, P:3 * P],
                                               inverse[:, r, 2 * hh + 1:2 * hh + 2], 1.0, ALU.mult, ALU.mult).then_inc(p_done, 1)
                    g = m - QL
                    if step_exists(J, g):
                        r = g % RING
                        need(pool, p_done, at_most(upto(J, m - IL, 2), 2 * B * NP))
                        need_alone(pool, qhi_done, upto(J, g, 2), spare_pool)
                        pool.tensor_scalar(q_lo[AT:AT + REST, r], f32(q_hi[0:REST, r]), 1.0, 1.0, ALU.mult, ALU.mult).then_inc(qdup_done, 1)
                        need(pool, qdup_done, upto(J, g))
                    g = m - PL
                    if step_exists(J, g):
                        r = g % RING
                        need(pool, p_done, at_most(upto(J, m - IL, 2), 2 * B * NP))
                        need_alone(pool, yhi_done, upto(J, g), spare_pool)
                        pool.tensor_scalar(y_lo[AT:AT + REST, r], f32(y_hi[0:REST, r]), 1.0, 1.0, ALU.mult, ALU.mult).then_inc(ydup_done, 1)
                        need(pool, ydup_done, upto(J, g))
                    if m % NP == NORM % NP and seq_exists(J, (m - NORM) // NP):
                        need(pool, ve_done, upto_seq(J, (m - NORM) // NP))
                        pool.tensor_tensor(rstd[:], var_eps[:], half[:], ALU.pow).then_inc(rstd_done, 1)

            over_bodies(pool, body, 1, BODIES, BODIES + 1)

        @block.tensor
        def _(pe):
            first_use = {QL + n * NP // WD_PARTS: (w_lo, n + 2) for n in range(WD_PARTS)} | {OL: (ow_done, OW_PARTS)}

            def body(J):
                for m in range(BODY):
                    if isinstance(J, int) and J == 0 and m in first_use:
                        pe.wait_ge(*first_use[m])
                    if m % NP == KV_MM and seq_exists(J, (m - KV_MM) // NP):
                        b = (m - KV_MM) // NP
                        need(pe, xlo_done, upto_seq(J, b))
                        need(pe, kv_done, upto_seq(J, b - 1))
                        for k in range(KC):
                            mm = three(pe, KV[:, 0:T], lw_hi[:, k], lw_lo[:, k], x_hi[:, b % 2, k], x_lo[:, b % 2, k],
                                       k == 0, k == KC - 1)
                        mm.then_inc(kvT_mm, 1)
                    g = m - SL
                    if step_exists(J, g):
                        r, b = g % RING, (g // NP) % 2
                        if g % NP == 0:
                            need(pe, kvTb_done, upto_seq(J, g // NP, 2))
                        need(pe, qdup_done, upto(J, g))
                        for hh in range(2):
                            need(pe, qlo_done, upto(J, g, 2, hh - 1))
                            need(pe, s_read, upto(J, g - 1, 4, 2 * hh - 2))
                            for t in range(TT):
                                tk = slice(t * P, t * P + P)
                                mm = two(pe, SC[hh][:, t * T:t * T + T], q_hi[:, r, hh, tk], q_lo[:, r, hh, tk],
                                         kvT_a[:, b], kvT_b[:, b], True, True)
                            mm.then_inc(s_mm, 1)
                    g = m - QL
                    if step_exists(J, g):
                        b, p = (g // NP) % 2, g % NP
                        if p == 0:
                            need(pe, xlo_done, upto_seq(J, g // NP))
                        need(pe, qlo_done, upto(J, g - 1, 2))
                        for hh in range(2):
                            w = slice((2 * p + hh) * P, (2 * p + hh + 1) * P)
                            for k in range(KC):
                                mm = three(pe, Q[:, hh * T:hh * T + T], wd_hi[:, k, w], wd_lo[:, k, w],
                                           x_hi[:, b, k], x_lo[:, b, k], k == 0, k == KC - 1)
                        mm.then_inc(q_mm, 1)
                    g = m - PL
                    if step_exists(J, g):
                        r, b = g % RING, (g // NP) % 2
                        if g % NP == 0:
                            need(pe, kv_done, upto_seq(J, g // NP))
                        need(pe, pTlo_done, upto(J, g, 2))
                        need(pe, ylo_done, upto(J, g - 1))
                        out = PV[:].rearrange("l (h t) -> l h t", h=2)
                        three(pe, out, kv_hi[:, b, 0], kv_lo[:, b, 0], pT_hi[:, r, :, 0:T], pT_lo[:, r, :, 0:T], True, False)
                        three(pe, out[:, :, P:T], kv_hi[:, b, 1], kv_lo[:, b, 1], pT_hi[:, r, :, T:3 * P],
                              pT_lo[:, r, :, T:3 * P], False, True).then_inc(pv_mm, 1)
                    g = m - TL
                    if step_exists(J, g):
                        r = g % RING
                        for hh in range(2):
                            need(pe, p_done, upto(J, g, 2, hh - 1))
                            need(pe, pTlo_done, upto(J, g - 1, 2, hh - 1))
                            for n in range(3):
                                mm = pe.transpose(TR[hh][:, n * P:n * P + P], prob[:, r, hh, n * P:n * P + P], ident[:])
                            mm.then_inc(p_tr, 1)
                    if m % NP == KV_TR and seq_exists(J, (m - KV_TR) // NP):
                        b = (m - KV_TR) // NP
                        need(pe, kvT_done, upto_seq(J, b, 3))
                        for t in range(TT):
                            mm = pe.transpose(KV[:, T + t * P:T + t * P + P], kvT[:, t * P:t * P + P], ident[:])
                        mm.then_inc(kv_tr, 1)
                    g = m - OL
                    if step_exists(J, g):
                        r, p = g % RING, g % NP
                        need(pe, ylo_done, upto(J, g))
                        need(pe, ydup_done, upto(J, g))
                        if p == 0:
                            need(pe, o_read, upto_seq(J, g // NP - 1))
                        for hh in range(2):
                            w = slice((2 * p + hh) * C, (2 * p + hh + 1) * C)
                            for t in range(TT):
                                tk = slice(t * P, t * P + P)
                                mm = two(pe, O[:, t * C:t * C + C], y_hi[:, r, hh, tk], y_lo[:, r, hh, tk], ow[:, 0, w],
                                         ow[:, 1, w], p == 0 and hh == 0 and t == 0, p == NP - 1 and hh == 1)
                        mm.then_inc(o_mm, 1)

            over_bodies(pe, body, 1, BODIES, BODIES + 1)

        @block.scalar
        def _(act):
            def split_wd(n):
                act.wait_ge(wd_in[n], 16)
                act.activation(wd_hi[:, :, wd_part(n)], wd_raw[:, :, wd_part(n)], ACT.Copy).then_inc(w_hi, 1)

            act.wait_ge(lw_in, 48)
            act.activation(lw_hi[:], lw_raw[:], ACT.Copy).then_inc(w_hi, 1)

            def body(J):
                for m in range(BODY):
                    if m % NP == 0 and seq_exists(J, m // NP):
                        b = m // NP
                        need(act, xT_in[b], J * 16 + 16)
                        need(act, q_mm, upto(J, (b - 1) * NP - 1))
                        act.activation(x_hi[:, b], xT_raw[:, b], ACT.Copy).then_inc(xhi_done, 1)
                        if isinstance(J, int) and J == 0 and m == 0:
                            split_wd(0)
                    if m % NP == KV_MM and seq_exists(J, (m - KV_MM) // NP):
                        b = (m - KV_MM) // NP
                        need(act, kvT_mm, upto_seq(J, b))
                        need(act, kv_tr, upto_seq(J, b - 1))
                        need(act, kvTb_done, upto_seq(J, b - 1, 2))
                        act.activation(kvT[:], KV[:, 0:T], ACT.Identity, bias=lbias[:, 0:1]).then_inc(kvT_done, 1)
                        need(act, s_mm, upto(J, (b - 1) * NP - 1, 2))
                        act.activation(kvT_a[:, b % 2], KV[:, 0:T], ACT.Identity, bias=lbias[:, 0:1]).then_inc(kvT_done, 1)
                        act.activation(kvT_b[0:L, b % 2], KV[0:L, 0:T], ACT.Identity, bias=lbias[0:L, 0:1]).then_inc(kvT_done, 1)
                    g = m - QL
                    if step_exists(J, g):
                        r, p = g % RING, g % NP
                        need(act, q_mm, upto(J, g))
                        need(act, s_mm, upto(J, g - RING, 2))
                        for hh in range(2):
                            h = 2 * p + hh
                            act.activation(q_hi[:, r, hh], Q[:, hh * T:hh * T + T], ACT.Identity,
                                           bias=qbias[:, h:h + 1]).then_inc(qhi_done, 1)
                    g = m - PL
                    if step_exists(J, g):
                        r = g % RING
                        need(act, pv_mm, upto(J, g))
                        if isinstance(J, int) and J == 0 and g == 0:
                            act.wait_ge(ow_done, OW_PARTS)
                        need(act, o_mm, upto(J, g - RING))
                        act.activation(y_hi[:, r].rearrange("l h t -> l (h t)"), PV[:], ACT.Copy).then_inc(yhi_done, 1)
                    g = m - TL
                    if step_exists(J, g):
                        r = g % RING
                        for hh in range(2):
                            need(act, p_tr, upto(J, g, 2, hh - 1))
                            if hh == 0:
                                need(act, pv_mm, upto(J, g - RING))
                            act.activation(pT_hi[:, r, hh], TR[hh][:, 0:3 * P], ACT.Copy).then_inc(pThi_done, 1)
                    if m % NP == KV_TR and seq_exists(J, (m - KV_TR) // NP):
                        b = (m - KV_TR) // NP
                        need(act, kv_tr, upto_seq(J, b))
                        need(act, pv_mm, upto(J, (b - 1) * NP - 1))
                        act.activation(kv_hi[:, b % 2].rearrange("p t l -> p (t l)"), KV[:, T:T + TT * P],
                                       ACT.Copy).then_inc(kvhi_done, 1)
                    g = m - SL
                    if step_exists(J, g):
                        r = g % RING
                        for hh in range(2):
                            for t in range(TT):
                                n = 2 * hh + t
                                need(act, s_read, upto(J, g, 4, n - 3))
                                cols = slice(0, P) if t == 0 else slice(P, 3 * P)
                                act.activation(prob[:, r, hh, cols], prob[:, r, hh, cols], ACT.Exp, bias=shift[:, r, n:n + 1],
                                               scale=-1.0, accum_out=total[:, r, n:n + 1]).then_inc(exp_done, 1)
                    if isinstance(J, int) and J == 0 and 0 < m < WD_PARTS:
                        split_wd(m)
                    if isinstance(J, int) and J == 0 and OW_FROM <= m < OW_FROM + OW_PARTS:
                        if m == OW_FROM:
                            act.wait_ge(ow_in, 48)
                        part = slice((m - OW_FROM) * OW_COLS, (m - OW_FROM + 1) * OW_COLS)
                        act.activation(ow_flat[:, part], ow_raw_flat[:, part], ACT.Copy).then_inc(owhi_done, 1)

            over_bodies(act, body, 1, BODIES, BODIES + 1)

        @block.vector
        def _(dve):
            def split_wd(n):
                at = (slice(None), slice(None), wd_part(n))
                dve.wait_ge(w_hi, n + 2)
                dve.tensor_tensor(wd_lo[at], wd_raw[at], f32(wd_hi[at]), ALU.subtract).then_inc(w_lo, 1)

            dve.wait_ge(w_hi, 1)
            dve.tensor_tensor(lw_lo[:], lw_raw[:], f32(lw_hi[:]), ALU.subtract).then_inc(w_lo, 1)
            dve.wait_ge(const, 7)

            def body(J):
                for m in range(BODY):
                    if m % NP == 0 and seq_exists(J, m // NP):
                        b = m // NP
                        need(dve, xhi_done, upto_seq(J, b))
                        dve.tensor_tensor(x_lo[:, b], xT_raw[:, b], f32(x_hi[:, b]), ALU.subtract).then_inc(xlo_done, 1)
                        if isinstance(J, int) and J == 0 and m == 0:
                            split_wd(0)
                    if m % NP == KV_MM and seq_exists(J, (m - KV_MM) // NP):
                        b = (m - KV_MM) // NP
                        need(dve, kvT_done, upto_seq(J, b, 3))
                        dve.tensor_tensor(kvT_b[AT:AT + REST, b % 2], kvT[0:REST, :], f32(kvT_b[0:REST, b % 2]),
                                          ALU.subtract).then_inc(kvTb_done, 1)
                        dve.scalar_tensor_tensor(out=kvT_a[:, b % 2], in0=f32(kvT_a[:, b % 2]), scalar=minus_low[:, 0:1], in1=kvT[:],
                                                 op0=ALU.mult, op1=ALU.add).then_inc(kvTb_done, 1)
                    if m % NP == NORM % NP and seq_exists(J, (m - NORM) // NP):
                        b = (m - NORM) // NP
                        need(dve, o_mm, upto(J, (b + 1) * NP - 1))
                        need(dve, xres_done, upto_seq(J, b, TT))
                        dve.tensor_tensor(res[:].rearrange("p t c -> p (t c)"), O[:, 0:TT * C],
                                          x_res[:, b % 2].rearrange("p t c -> p (t c)"), ALU.add).then_inc(o_read, 1)
                    g = m - SL
                    if step_exists(J, g):
                        r = g % RING
                        need(dve, p_tr, upto(J, g - RING, 2))
                        for hh in range(2):
                            need_alone(dve, s_mm, upto(J, g, 2, hh - 1), spare_dve)
                            for t in range(TT):
                                n = 2 * hh + t
                                cols = slice(0, P) if t == 0 else slice(P, 3 * P)
                                dve.tensor_tensor_reduce(
                                    out=prob[:, r, hh, cols], in0=SC[hh][:, t * T:t * T + (t + 1) * P],
                                    in1=mask[:].rearrange("p a s -> p (a s)")[:, cols], scale=-SELF_SCALE, scalar=-MASKED,
                                    op0=ALU.add, op1=ALU.min, accum_out=shift[:, r, n:n + 1]).then_inc(s_read, 1)
                    g = m - IL
                    if step_exists(J, g):
                        r = g % RING
                        need(dve, exp_done, upto(J, g, 4))
                        dve.reciprocal(inverse[:, r], total[:, r]).then_inc(inv_done, 1)
                    g = m - QL
                    if step_exists(J, g):
                        r, p = g % RING, g % NP
                        need(dve, qhi_done, upto(J, g, 2))
                        for hh in range(2):
                            h = 2 * p + hh
                            dve.scalar_tensor_tensor(out=q_lo[0:AT, r, hh], in0=Q[0:AT, hh * T:hh * T + T], scalar=qbias[0:AT, h:h + 1],
                                                     in1=f32(q_hi[0:AT, r, hh]), op0=ALU.add, op1=ALU.subtract).then_inc(qlo_done, 1)
                    g = m - PL
                    if step_exists(J, g):
                        r = g % RING
                        need(dve, yhi_done, upto(J, g))
                        dve.tensor_tensor(y_lo[0:AT, r].rearrange("l h t -> l (h t)"), PV[0:AT, :],
                                          f32(y_hi[0:AT, r].rearrange("l h t -> l (h t)")), ALU.subtract).then_inc(ylo_done, 1)
                    g = m - TL
                    if step_exists(J, g):
                        r = g % RING
                        for hh in range(2):
                            need(dve, pThi_done, upto(J, g, 2, hh - 1))
                            dve.tensor_tensor(pT_lo[:, r, hh], TR[hh][:, 0:3 * P], f32(pT_hi[:, r, hh]),
                                              ALU.subtract).then_inc(pTlo_done, 1)
                    if m % NP == KV_TR and seq_exists(J, (m - KV_TR) // NP):
                        b = (m - KV_TR) // NP
                        need(dve, kvhi_done, upto_seq(J, b))
                        dve.tensor_tensor(kv_lo[:, b % 2].rearrange("p t l -> p (t l)"), KV[:, T:T + TT * P],
                                          f32(kv_hi[:, b % 2].rearrange("p t l -> p (t l)")), ALU.subtract).then_inc(kv_done, 1)
                    if m % NP == (NORM + 1) % NP and seq_exists(J, (m - NORM - 1) // NP):
                        b = (m - NORM - 1) // NP
                        need(dve, rstd_done, upto_seq(J, b))
                        need(dve, x1_out[b % 2], J * 16 + 16 * (b // 2))
                        for t in range(TT):
                            ins = dve.tensor_scalar(x1[:, b % 2, t], res[:, t], meanvar[:, t, 0:1], rstd[:, t:t + 1],
                                                    ALU.subtract, ALU.mult)
                        ins.then_inc(x1_done, 1)
                    if m % NP == NORM % NP and seq_exists(J, (m - NORM) // NP):
                        b = (m - NORM) // NP
                        need(dve, o_read, upto_seq(J, b))
                        for t in range(TT):
                            dve.bn_stats(stats[:, t], res[:, t]).then_inc(st_done, 1)
                        need_alone(dve, st_done, upto_seq(J, b, TT), spare_dve)
                        for t in range(TT):
                            dve.bn_aggr(meanvar[:, t], stats[:, t]).then_inc(mv_done, 1)
                        need(dve, mv_done, upto_seq(J, b, TT))
                        dve.tensor_scalar(var_eps[:], meanvar[:, :, 1], EPS, None, ALU.add).then_inc(ve_done, 1)
                    if isinstance(J, int) and J == 0 and 0 < m < WD_PARTS:
                        split_wd(m)
                    if isinstance(J, int) and J == 0 and OW_FROM <= m < OW_FROM + OW_PARTS:
                        part = slice((m - OW_FROM) * OW_COLS, (m - OW_FROM + 1) * OW_COLS)
                        dve.wait_ge(owhi_done, m - OW_FROM + 1)
                        dve.scalar_tensor_tensor(out=ow_flat[:, part], in0=f32(ow_flat[:, part]), scalar=minus_low[:, 0:1],
                                                 in1=ow_raw_flat[:, part], op0=ALU.mult, op1=ALU.add).then_inc(ow_done, 1)

            over_bodies(dve, body, 1, BODIES, BODIES + 1)




def cross_attention(nc, bank, ident, logits, wv_raw, wv_in, d):
    with ExitStack() as ctx:
        al = Alloc(nc, ctx, "ca")
        names = ("wv", "wq", "wk", "wo")
        shapes = {"wq": [P, KC, H * DH], "wk": [P, KC, H * DH], "wv": [P, KC, H * DH], "wo": [P, NP, C]}
        w = {n: al.split(n, shapes[n]) for n in names}
        gate_hi, gate_lo = al.split("gate", [P, KC, E])
        gate_raw = al.sb("gate_raw", [P, KC, E])
        half = al.sb("half", [P, TT])
        x_raw = al.sb("x_raw", [P, 2, TT, C])
        x_res = al.sb("x_res", [P, TT, C])
        xT_hi, xT_lo = al.split("xT", [P, 2, KC, T])
        cT_raw = al.sb("cT_raw", [P, KC, 2, S])
        cT_hi, cT_lo = al.split("cT", [P, KC, 2, S])
        q_hi, q_lo = al.split("q", [P, RING, T])
        prob = al.sb("prob", [P, RING, TT, 2, S])
        shift = al.sb("shift", [P, RING, TT * 2])
        total = al.sb("total", [P, RING, TT * 2])
        inverse = al.sb("inverse", [P, RING, TT * 2])
        pT_hi, pT_lo = al.split("pT", [S, RING, 2, T])
        c_hi, c_lo = al.split("c", [P, RING, T])
        res = al.sb("res", [P, TT, C])
        stats, meanvar = al.sb("stats", [P, TT, 6]), al.sb("meanvar", [P, TT, 2])
        var_eps, rstd = al.sb("var_eps", [P, TT]), al.sb("rstd", [P, TT])
        x2 = al.sb("x2", [P, 2, TT, C])
        x2T_hi, x2T_lo = al.split("x2T", [P, KC, T])
        with ExitStack() as first:
            raw = [wv_raw[:].rearrange("p k n -> p (k n)")] + [
                first.enter_context(nc.sbuf_tensor(f"ca_{n}_raw", [P, KC * H * DH], F32))[:] for n in names[1:]]
        k_hi, k_lo = al.split("k", [P, 2, NP, 2 * S])
        v_hi, v_lo = al.split("v", [S, 2, NP, 3 * DH])

        SC, QK, TR, CX, O, XT, M = bank[0:2], *bank[2:8]
        Q, K = QK[:, 0:T], QK[:, T:T + 2 * S]

        w_in = [wv_in] + [al.sem(f"{n}_in") for n in names[1:]]
        w_hi, w_lo, const = al.sem("w_hi"), al.sem("w_lo"), al.sem("const")
        gate_in = al.sem("gate_in")
        x_in = [al.sem(f"x_in{i}") for i in range(2)]
        c_in, res_in = al.sem("c_in"), al.sem("res_in")
        x2_out = [al.sem(f"x2_out{i}") for i in range(2)]
        chi_done, clo_done = al.sem("chi_done"), al.sem("clo_done")
        x_tr, xThi_done, xTlo_done = al.sem("x_tr"), al.sem("xThi_done"), al.sem("xTlo_done")
        v_mm, vhi_done, vlo_done = al.sem("v_mm"), al.sem("vhi_done"), al.sem("vlo_done")
        k_mm, khi_done, klo_done = al.sem("k_mm"), al.sem("khi_done"), al.sem("klo_done")
        q_mm, qhi_done, qlo_done = al.sem("q_mm"), al.sem("qhi_done"), al.sem("qlo_done")
        s_mm, max_done, exp_done = al.sem("s_mm"), al.sem("max_done"), al.sem("exp_done")
        inv_done, p_done = al.sem("inv_done"), al.sem("p_done")
        p_tr, pThi_done, pTlo_done = al.sem("p_tr"), al.sem("pThi_done"), al.sem("pTlo_done")
        cx_mm, cxhi_done, cxlo_done = al.sem("cx_mm"), al.sem("cxhi_done"), al.sem("cxlo_done")
        o_mm, o_read = al.sem("o_mm"), al.sem("o_read")
        st_done, mv_done, ve_done, rstd_done, x2_done = (
            al.sem("st_done"), al.sem("mv_done"), al.sem("ve_done"), al.sem("rstd_done"), al.sem("x2_done"))
        x2_tr, x2Thi_done, x2Tlo_done = al.sem("x2_tr"), al.sem("x2Thi_done"), al.sem("x2Tlo_done")
        g_mm, g_done = al.sem("g_mm"), al.sem("g_done")
        spare_dve, spare_pool, spare_act = al.sem("spare_dve"), al.sem("spare_pool"), al.sem("spare_act")

        QL, SL, IL, TL, CL, OL = 2, 4, 5, 6, 8, 10
        NORM, X2T, GATE = 18, 20, 21

        block = ctx.enter_context(nc.Block())

        @block.sync
        def _(sp):
            def body(J):
                if seq_exists(J, 0):
                    need(sp, clo_done, J)
                    for i in range(2):
                        sp.dma_start(cT_raw[:, :, i], d["ctxT"][J * 2 + i].rearrange("(k p) s -> p k s", p=P)).then_inc(c_in, 16)
                for i in range(2):
                    if seq_exists(J, i):
                        need(sp, x_tr, upto_seq(J, i - 2))
                        sp.dma_start(x_raw[:, i], d["x1"][J * 2 + i].rearrange("(t p) c -> p t c", p=P)).then_inc(x_in[i], 16)
                    if isinstance(J, int) and J == 0:
                        for n in (1, 2) if i == 0 else (3,):
                            src = d[names[n]].rearrange("(k p) n -> p k n", p=P) if n < 3 else d[names[n]].rearrange("p (k n) -> p k n", k=NP)
                            sp.dma_start(raw[n].rearrange("p (k n) -> p k n", k=shapes[names[n]][1]), src).then_inc(w_in[n], 16)
                        if i == 1:
                            sp.dma_start(gate_raw[:], d["gate"].rearrange("(k p) e -> p k e", p=P)).then_inc(gate_in, 16)
                    if seq_exists(J, i - 2):
                        need(sp, o_read, upto_seq(J, i - 3))
                        sp.dma_start(x_res[:], d["x1"][J * 2 + (i - 2)].rearrange("(t p) c -> p t c", p=P)).then_inc(res_in, 16)
                    if seq_exists(J, i - 3):
                        k = (i - 3) % 2
                        need(sp, x2_done, upto_seq(J, i - 3))
                        sp.dma_start(d["x2"][J * 2 + (i - 3)].rearrange("(t p) c -> p t c", p=P), x2[:, k]).then_inc(x2_out[k], 16)

            over_bodies(sp, body, 2, BODIES, BODIES + 2)
            for i in range(2):
                sp.wait_ge(x2_out[i], 16 * BODIES)

        @block.gpsimd
        def _(pool):
            pool.memset(half[:], -0.5).then_inc(const, 1)
            zeros = [k_hi[0:DH, :, :, S:2 * S], k_lo[0:DH, :, :, S:2 * S], k_hi[DH:P, :, :, 0:S], k_lo[DH:P, :, :, 0:S],
                     v_hi[:, :, :, DH:2 * DH], v_lo[:, :, :, DH:2 * DH]]
            pool.wait_ge(w_lo, len(names))
            for n, t in enumerate(zeros):
                pool.wait_ge(const, n + 1)
                pool.memset(f32(t), 0.0).then_inc(const, 1)
            pool.wait_ge(const, 7)

            def body(J):
                for m in range(BODY):
                    g = m - IL
                    if step_exists(J, g):
                        r = g % RING
                        need_alone(pool, inv_done, upto(J, g), spare_pool)
                        for t in range(TT):
                            for hh in range(2):
                                n = 2 * t + hh
                                ins = pool.tensor_scalar(prob[:, r, t, hh], prob[:, r, t, hh], inverse[:, r, n:n + 1], 1.0,
                                                         ALU.mult, ALU.mult)
                        ins.then_inc(p_done, 1)
                    if m % NP == NORM % NP and seq_exists(J, (m - NORM) // NP):
                        need(pool, ve_done, upto_seq(J, (m - NORM) // NP))
                        pool.tensor_tensor(rstd[:], var_eps[:], half[:], ALU.pow).then_inc(rstd_done, 1)

            over_bodies(pool, body, 1, BODIES, BODIES + 1)

        @block.tensor
        def _(pe):
            first_use = {1: (w_lo, 1), QL: (w_lo, 3), SL: (const, 7), OL: (w_lo, 5)}

            def body(J):
                for m in range(BODY):
                    if isinstance(J, int) and J == 0 and m in first_use:
                        pe.wait_ge(*first_use[m])
                    if m % NP == 0 and seq_exists(J, m // NP):
                        b = m // NP
                        need(pe, x_in[b], J * 16 + 16)
                        need(pe, x2Tlo_done, upto_seq(J, b - 3))
                        need(pe, xTlo_done, upto_seq(J, b - 1))
                        for k in range(KC):
                            for t in range(TT):
                                mm = pe.transpose(XT[:, k * T + t * P:k * T + t * P + P], x_raw[:, b, t, k * P:k * P + P], ident[:])
                        mm.then_inc(x_tr, 1)
                    if m % NP in (1, 2) and seq_exists(J, m // NP):
                        b, n = m // NP, m % NP - 1
                        need(pe, clo_done, J + 1)
                        need(pe, vlo_done, upto_seq(J, b, 2, n - 2))
                        need(pe, g_done, upto_seq(J, b - 3))
                        for k in range(KC):
                            half_n = slice(n * 512, n * 512 + 512)
                            mm = three(pe, M[0:S, :], cT_hi[:, k, b], cT_lo[:, k, b], w["wv"][0][:, k, half_n],
                                       w["wv"][1][:, k, half_n], k == 0, k == KC - 1)
                        mm.then_inc(v_mm, 1)
                    g = m - SL
                    if step_exists(J, g):
                        r, b, p = g % RING, (g // NP) % 2, g % NP
                        need(pe, qlo_done, upto(J, g))
                        if b == 0:
                            need(pe, klo_done, J * NP + p + 1 if g >= 0 else J * NP + p + 1 - NP)
                        need(pe, exp_done, upto(J, g - 2, 4))
                        for t in range(TT):
                            tk = slice(t * P, t * P + P)
                            mm = three(pe, SC[g % 2][:, t * 2 * S:(t + 1) * 2 * S], q_hi[:, r, tk], q_lo[:, r, tk], k_hi[:, b, p],
                                       k_lo[:, b, p], True, True)
                        mm.then_inc(s_mm, 1)
                    g = m - QL
                    if step_exists(J, g):
                        b, p = (g // NP) % 2, g % NP
                        if p == 0:
                            need(pe, xTlo_done, upto_seq(J, g // NP))
                        need(pe, qlo_done, upto(J, g - 1))
                        ws = slice(p * P, p * P + P)
                        if b == 1 and p == 0 and g >= 0:
                            need(pe, klo_done, J * NP + NP)
                        if b == 0:
                            jk = J * NP + p + 1
                            need(pe, clo_done, J + 1)
                            need(pe, klo_done, jk - 1)
                            for k in range(KC):
                                mm = three(pe, K, w["wk"][0][:, k, ws], w["wk"][1][:, k, ws],
                                           cT_hi[:, k].rearrange("p b s -> p (b s)"), cT_lo[:, k].rearrange("p b s -> p (b s)"),
                                           k == 0, k == KC - 1)
                            mm.then_inc(k_mm, 1)
                        for k in range(KC):
                            mm = three(pe, Q, w["wq"][0][:, k, ws], w["wq"][1][:, k, ws], xT_hi[:, b, k], xT_lo[:, b, k],
                                       k == 0, k == KC - 1)
                        mm.then_inc(q_mm, 1)
                    g = m - CL
                    if step_exists(J, g):
                        r, b, p = g % RING, (g // NP) % 2, g % NP
                        if p == 0:
                            need(pe, vlo_done, upto_seq(J, g // NP, 2))
                        need(pe, pTlo_done, upto(J, g))
                        need(pe, cxlo_done, upto(J, g - 1))
                        for hh in range(2):
                            win = slice(hh * DH, hh * DH + 2 * DH)
                            mm = three(pe, CX[:, 0:T], v_hi[:, b, p, win], v_lo[:, b, p, win], pT_hi[:, r, hh], pT_lo[:, r, hh],
                                       hh == 0, hh == 1)
                        mm.then_inc(cx_mm, 1)
                    g = m - TL
                    if step_exists(J, g):
                        r = g % RING
                        need(pe, p_done, upto(J, g))
                        need(pe, pTlo_done, upto(J, g - 1))
                        for hh in range(2):
                            for t in range(TT):
                                mm = pe.transpose(TR[0:S, hh * T + t * P:hh * T + t * P + P], prob[:, r, t, hh], ident[:])
                        mm.then_inc(p_tr, 1)
                    if m % NP == X2T % NP and seq_exists(J, (m - X2T) // NP):
                        b = (m - X2T) // NP
                        need(pe, x2_done, upto_seq(J, b))
                        need(pe, xTlo_done, at_most(upto_seq(J, b + 2), B))
                        for k in range(KC):
                            for t in range(TT):
                                mm = pe.transpose(XT[:, k * T + t * P:k * T + t * P + P], x2[:, b % 2, t, k * P:k * P + P], ident[:])
                        mm.then_inc(x2_tr, 1)
                    if m % NP == GATE % NP and seq_exists(J, (m - GATE) // NP):
                        b = (m - GATE) // NP
                        need(pe, x2Tlo_done, upto_seq(J, b))
                        need(pe, vlo_done, at_most(upto_seq(J, b + 2, 2), 2 * B))
                        for t in range(TT):
                            tk = slice(t * P, t * P + P)
                            for k in range(KC):
                                mm = three(pe, M[:, t * E:t * E + E], x2T_hi[:, k, tk], x2T_lo[:, k, tk], gate_hi[:, k],
                                           gate_lo[:, k], k == 0, k == KC - 1)
                        mm.then_inc(g_mm, 1)
                    g = m - OL
                    if step_exists(J, g):
                        r, p = g % RING, g % NP
                        need(pe, cxlo_done, upto(J, g))
                        if p == 0:
                            need(pe, o_read, upto_seq(J, g // NP - 1))
                        for t in range(TT):
                            tk = slice(t * P, t * P + P)
                            mm = three(pe, O[:, t * C:t * C + C], c_hi[:, r, tk], c_lo[:, r, tk], w["wo"][0][:, p], w["wo"][1][:, p],
                                       p == 0 and t == 0, p == NP - 1)
                        mm.then_inc(o_mm, 1)

            over_bodies(pe, body, 1, BODIES, BODIES + 1)

        @block.scalar
        def _(act):
            def split(n):
                act.wait_ge(w_in[n], 16)
                act.activation(w[names[n]][0][:].rearrange("p k n -> p (k n)"), raw[n], ACT.Copy,
                               scale=CROSS_SCALE if names[n] == "wq" else 1.0).then_inc(w_hi, 1)

            split(0)

            def body(J):
                for m in range(BODY):
                    if m == 0 and seq_exists(J, 0):
                        need(act, c_in, J * 32 + 32)
                        need(act, v_mm, J * 4)
                        need(act, k_mm, J * NP)
                        act.activation(cT_hi[:], cT_raw[:], ACT.Copy).then_inc(chi_done, 1)
                    if m % NP == 0 and seq_exists(J, m // NP):
                        b = m // NP
                        need(act, x_tr, upto_seq(J, b))
                        need(act, q_mm, upto(J, (b - 1) * NP - 1))
                        act.activation(xT_hi[:, b].rearrange("p k t -> p (k t)"), XT[:], ACT.Copy).then_inc(xThi_done, 1)
                    if isinstance(J, int) and J == 0 and m == 0:
                        split(1)
                        split(2)
                    if isinstance(J, int) and J == 0 and m == 2:
                        split(3)
                        act.wait_ge(gate_in, 16)
                        act.activation(gate_hi[:], gate_raw[:], ACT.Copy).then_inc(w_hi, 1)
                        act.wait_ge(w_lo, 4)
                    if m % NP in (1, 2) and seq_exists(J, m // NP):
                        b, n = m // NP, m % NP - 1
                        need(act, v_mm, upto_seq(J, b, 2, n - 1))
                        if n == 0:
                            need(act, cx_mm, upto(J, (b - 1) * NP - 1))
                        for hh in range(2):
                            ins = act.activation(v_hi[:, b, n * NP // 2:(n + 1) * NP // 2, hh * 2 * DH:hh * 2 * DH + DH],
                                                 M[0:S, :].rearrange("s (p h k) -> s p h k", h=2, k=DH)[:, :, hh], ACT.Copy)
                        ins.then_inc(vhi_done, 1)
                    g = m - QL
                    if step_exists(J, g):
                        r, b, p = g % RING, (g // NP) % 2, g % NP
                        need(act, q_mm, upto(J, g))
                        need(act, s_mm, upto(J, g - RING))
                        act.activation(q_hi[:, r], Q, ACT.Copy).then_inc(qhi_done, 1)
                        if b == 0:
                            jk = J * NP + p + 1
                            need(act, k_mm, jk)
                            need(act, s_mm, upto(J, g - NP))
                            for hh in range(2):
                                rows = slice(hh * DH, hh * DH + DH)
                                ins = act.activation(k_hi[rows, :, p, hh * S:hh * S + S],
                                                     QK[rows, T:T + 2 * S].rearrange("k (b s) -> k b s", b=2), ACT.Copy)
                            ins.then_inc(khi_done, 1)
                    g = m - CL
                    if step_exists(J, g):
                        r = g % RING
                        need(act, cx_mm, upto(J, g))
                        need(act, o_mm, upto(J, g - RING))
                        act.activation(c_hi[:, r], CX[:, 0:T], ACT.Copy).then_inc(cxhi_done, 1)
                    g = m - TL
                    if step_exists(J, g):
                        r = g % RING
                        need(act, p_tr, upto(J, g))
                        need(act, cx_mm, upto(J, g - RING))
                        act.activation(pT_hi[:, r].rearrange("s h t -> s (h t)"), TR[0:S, :], ACT.Copy).then_inc(pThi_done, 1)
                    if m % NP == X2T % NP and seq_exists(J, (m - X2T) // NP):
                        b = (m - X2T) // NP
                        need(act, x2_tr, upto_seq(J, b))
                        need(act, g_mm, upto_seq(J, b - 1))
                        act.activation(x2T_hi[:].rearrange("p k t -> p (k t)"), XT[:], ACT.Copy).then_inc(x2Thi_done, 1)
                    if m % NP == GATE % NP and seq_exists(J, (m - GATE) // NP):
                        b = (m - GATE) // NP
                        need_alone(act, g_mm, upto_seq(J, b), spare_act)
                        act.activation(logits[:, J * 2 + b].rearrange("p t e -> p (t e)"), M[:, 0:TT * E], ACT.Copy).then_inc(g_done, 1)
                    g = m - SL
                    if step_exists(J, g):
                        r = g % RING
                        need(act, max_done, upto(J, g))
                        need(act, p_tr, upto(J, g - RING))
                        for t in range(TT):
                            for hh in range(2):
                                n = 2 * t + hh
                                act.activation(prob[:, r, t, hh], SC[g % 2][:, n * S:n * S + S], ACT.Exp, bias=shift[:, r, n:n + 1],
                                               accum_out=total[:, r, n:n + 1]).then_inc(exp_done, 1)

            over_bodies(act, body, 1, BODIES, BODIES + 1)

        @block.vector
        def _(dve):
            def split(n):
                dve.wait_ge(w_hi, n + 1)
                hi, lo = (t[:].rearrange("p k n -> p (k n)") for t in w[names[n]])
                dve.scalar_tensor_tensor(out=lo, in0=raw[n], scalar=CROSS_SCALE if names[n] == "wq" else 1.0, in1=f32(hi),
                                         op0=ALU.mult, op1=ALU.subtract).then_inc(w_lo, 1)

            split(0)

            def body(J):
                for m in range(BODY):
                    if m == 0 and seq_exists(J, 0):
                        need(dve, chi_done, J + 1)
                        dve.tensor_tensor(cT_lo[:], cT_raw[:], f32(cT_hi[:]), ALU.subtract).then_inc(clo_done, 1)
                    if m % NP == 0 and seq_exists(J, m // NP):
                        b = m // NP
                        need(dve, xThi_done, upto_seq(J, b))
                        dve.tensor_tensor(xT_lo[:, b].rearrange("p k t -> p (k t)"), XT[:],
                                          f32(xT_hi[:, b].rearrange("p k t -> p (k t)")), ALU.subtract).then_inc(xTlo_done, 1)
                    if isinstance(J, int) and J == 0 and m == 0:
                        split(1)
                        split(2)
                    if isinstance(J, int) and J == 0 and m == 2:
                        split(3)
                        dve.wait_ge(w_hi, 5)
                        dve.tensor_tensor(gate_lo[:], gate_raw[:], f32(gate_hi[:]), ALU.subtract).then_inc(w_lo, 1)
                        dve.wait_ge(w_lo, 4)
                    if m % NP in (1, 2) and seq_exists(J, m // NP):
                        b, n = m // NP, m % NP - 1
                        need(dve, vhi_done, upto_seq(J, b, 2, n - 1))
                        for hh in range(2):
                            at = (slice(None), b, slice(n * NP // 2, (n + 1) * NP // 2), slice(hh * 2 * DH, hh * 2 * DH + DH))
                            ins = dve.tensor_tensor(v_lo[at], M[0:S, :].rearrange("s (p h k) -> s p h k", h=2, k=DH)[:, :, hh],
                                                    f32(v_hi[at]), ALU.subtract)
                        ins.then_inc(vlo_done, 1)
                    if m % NP == NORM % NP and seq_exists(J, (m - NORM) // NP):
                        b = (m - NORM) // NP
                        need(dve, o_mm, upto(J, (b + 1) * NP - 1))
                        need(dve, res_in, J * 32 + 16 * (b + 1))
                        dve.tensor_tensor(res[:].rearrange("p t c -> p (t c)"), O[:, 0:TT * C],
                                          x_res[:].rearrange("p t c -> p (t c)"), ALU.add).then_inc(o_read, 1)
                    g = m - SL
                    if step_exists(J, g):
                        r = g % RING
                        need(dve, s_mm, upto(J, g))
                        dve.tensor_reduce(shift[:, r], SC[g % 2][:, 0:TT * 2 * S].rearrange("p (n s) -> p n s", s=S), AXIS.X, ALU.max,
                                          negate=True).then_inc(max_done, 1)
                    g = m - IL
                    if step_exists(J, g):
                        r = g % RING
                        need(dve, exp_done, upto(J, g, 4))
                        dve.reciprocal(inverse[:, r], total[:, r]).then_inc(inv_done, 1)
                    g = m - QL
                    if step_exists(J, g):
                        r, b, p = g % RING, (g // NP) % 2, g % NP
                        need(dve, qhi_done, upto(J, g))
                        if b == 0:
                            need(dve, khi_done, J * NP + p + 1)
                        dve.tensor_tensor(q_lo[:, r], Q, f32(q_hi[:, r]), ALU.subtract).then_inc(qlo_done, 1)
                        if b == 0:
                            jk = J * NP + p + 1
                            for hh in range(2):
                                at = (slice(hh * DH, hh * DH + DH), slice(None), p, slice(hh * S, hh * S + S))
                                ins = dve.tensor_tensor(k_lo[at], QK[hh * DH:hh * DH + DH, T:T + 2 * S].rearrange("k (b s) -> k b s", b=2),
                                                        f32(k_hi[at]), ALU.subtract)
                            ins.then_inc(klo_done, 1)
                    g = m - CL
                    if step_exists(J, g):
                        r = g % RING
                        need(dve, cxhi_done, upto(J, g))
                        dve.tensor_tensor(c_lo[:, r], CX[:, 0:T], f32(c_hi[:, r]), ALU.subtract).then_inc(cxlo_done, 1)
                    g = m - TL
                    if step_exists(J, g):
                        r = g % RING
                        need(dve, pThi_done, upto(J, g))
                        dve.tensor_tensor(pT_lo[:, r].rearrange("s h t -> s (h t)"), TR[0:S, :],
                                          f32(pT_hi[:, r].rearrange("s h t -> s (h t)")), ALU.subtract).then_inc(pTlo_done, 1)
                    if m % NP == (NORM + 1) % NP and seq_exists(J, (m - NORM - 1) // NP):
                        b = (m - NORM - 1) // NP
                        need(dve, rstd_done, upto_seq(J, b))
                        need(dve, x2_out[b % 2], J * 16 + 16 * (b // 2))
                        for t in range(TT):
                            ins = dve.tensor_scalar(x2[:, b % 2, t], res[:, t], meanvar[:, t, 0:1], rstd[:, t:t + 1],
                                                    ALU.subtract, ALU.mult)
                        ins.then_inc(x2_done, 1)
                    if m % NP == NORM % NP and seq_exists(J, (m - NORM) // NP):
                        b = (m - NORM) // NP
                        need(dve, o_read, upto_seq(J, b))
                        for t in range(TT):
                            dve.bn_stats(stats[:, t], res[:, t]).then_inc(st_done, 1)
                        need_alone(dve, st_done, upto_seq(J, b, TT), spare_dve)
                        for t in range(TT):
                            dve.bn_aggr(meanvar[:, t], stats[:, t]).then_inc(mv_done, 1)
                        need(dve, mv_done, upto_seq(J, b, TT))
                        dve.tensor_scalar(var_eps[:], meanvar[:, :, 1], EPS, None, ALU.add).then_inc(ve_done, 1)
                    if m % NP == X2T % NP and seq_exists(J, (m - X2T) // NP):
                        b = (m - X2T) // NP
                        need(dve, x2Thi_done, upto_seq(J, b))
                        dve.tensor_tensor(x2T_lo[:].rearrange("p k t -> p (k t)"), XT[:],
                                          f32(x2T_hi[:].rearrange("p k t -> p (k t)")), ALU.subtract).then_inc(x2Tlo_done, 1)

            over_bodies(dve, body, 1, BODIES, BODIES + 1)




def route(nc, bank, ident, logits, index_col, weight_col, token_of, ahead, d):
    with ExitStack() as ctx:
        al = Alloc(nc, ctx, "rt")
        n_rows = B * TT
        best, total, inverse = al.sb("best", [P, n_rows]), al.sb("total", [P, n_rows]), al.sb("inverse", [P, n_rows])
        ex = al.sb("ex", [P, n_rows, E])
        score = al.sb("score", [P, TT, B * E])
        left = al.sb("left", [P, NG, T])
        value, index = al.sb("value", [P, NG, CAP]), al.sb("index", [P, NG, CAP], U32)
        index_f = al.sb("index_f", [P, NG, CAP])
        first_token = al.sb("first_token", [CAP, Q4, NG, GB // Q4])

        soft, exp_done = al.sem("soft"), al.sem("exp_done")
        s_tr, left_done = al.sem("s_tr"), al.sem("left_done")
        top, found, as_float = al.sem("top"), al.sem("found"), al.sem("as_float")
        i_tr, v_tr, col_done, weights_done = al.sem("i_tr"), al.sem("v_tr"), al.sem("col_done"), al.sem("weights_done")

        const, split_done = al.sem("const"), al.sem("split_done")

        block = ctx.enter_context(nc.Block())

        def bc(ap):
            return ap.rearrange("p (n o) -> p n o", o=1).broadcast_to([P, ap.shape[1], E])

        @block.sync
        def _(sp):
            for e in range(2):
                load_expert(sp, ahead, e, d, e)
            for (raw, _, _), name in zip(ahead.shared, ("sg", "su", "sd")):
                sp.dma_start(raw[:], d[name].rearrange("(k p) n -> p k n", p=P)).then_inc(ahead.shared_in, 16)

        @block.gpsimd
        def _(pool):
            for q in range(Q4):
                pool.iota(first_token[:, q], pattern=[[T * GB, NG], [T * Q4, GB // Q4]], base=T * q, channel_multiplier=0,
                          allow_small_or_imprecise_dtypes=True).then_inc(const, 1)
            for e in range(2):
                pool.wait_ge(ahead.whi_done, e + 1)
                for part in range(N_W // 512):
                    at = slice(part * 512, part * 512 + 512)
                    ins = pool.tensor_tensor(ahead.w_lo[:, e, at], ahead.w_raw[:, e, at], f32(ahead.w_hi[:, e, at]), ALU.subtract)
                ins.then_inc(ahead.wlo_done, 1)
            for n, (raw, hi, lo) in enumerate(ahead.shared):
                pool.wait_ge(ahead.shared_hi, n + 1)
                pool.tensor_tensor(lo[:], raw[:], f32(hi[:]), ALU.subtract).then_inc(split_done, 1)

        @block.scalar
        def _(act):
            act.wait_ge(soft, 2)
            act.activation(ex[:], ex[:], ACT.Exp).then_inc(exp_done, 1)
            for e in range(2):
                act.wait_ge(ahead.w_in[e], 48)
                act.activation(ahead.w_hi[:, e], ahead.w_raw[:, e], ACT.Copy).then_inc(ahead.whi_done, 1)
            act.wait_ge(ahead.shared_in, 48)
            for raw, hi, _ in ahead.shared:
                act.activation(hi[:], raw[:], ACT.Copy).then_inc(ahead.shared_hi, 1)
            act.wait_ge(v_tr, 1)
            for q in range(Q4):
                act.activation(weight_col[q * CAP:(q + 1) * CAP].rearrange("c b k o -> c b (k o)"),
                               bank[3][0:CAP].rearrange("c (b k q) -> c q b k", k=KS, q=Q4)[:, q], ACT.Copy).then_inc(weights_done, 1)

        @block.tensor
        def _(pe):
            pe.wait_ge(soft, 5)
            for g in range(NG):
                for t in range(TT):
                    at = (g % 2) * T + t * P
                    mm = pe.transpose(bank[g // 2][:, at:at + P], score[:, t, g * P:g * P + P], ident[:])
                if g % 2:
                    mm.then_inc(s_tr, 1)
            pe.wait_ge(found, NG * (CAP // 8))
            for g in range(NG):
                mm = pe.transpose(bank[3][0:CAP, g * P:g * P + P], value[:, g], ident[:])
            mm.then_inc(v_tr, 1)
            pe.wait_ge(as_float, 1)
            for g in range(NG):
                mm = pe.transpose(bank[2][0:CAP, g * P:g * P + P], index_f[:, g], ident[:])
            mm.then_inc(i_tr, 1)

        @block.vector
        def _(dve):
            rows_of = logits[:].rearrange("p b t e -> p (b t) e")
            dve.tensor_reduce(best[:], rows_of, AXIS.X, ALU.max).then_inc(soft, 1)
            dve.wait_ge(soft, 1)
            dve.tensor_tensor(ex[:], rows_of, bc(best[:]), ALU.subtract).then_inc(soft, 1)
            dve.wait_ge(exp_done, 1)
            dve.tensor_reduce(total[:], ex[:], AXIS.X, ALU.add).then_inc(soft, 1)
            dve.wait_ge(soft, 3)
            dve.reciprocal(inverse[:], total[:]).then_inc(soft, 1)
            dve.wait_ge(soft, 4)
            for t in range(TT):
                ins = dve.tensor_tensor(score[:, t].rearrange("p (b e) -> p b e", e=E),
                                        ex[:].rearrange("p (b t) e -> p b t e", t=TT)[:, :, t],
                                        bc(inverse[:]).rearrange("p (b t) e -> p b t e", t=TT)[:, :, t], ALU.mult)
            ins.then_inc(soft, 1)
            for n in range(NG // 2):
                dve.wait_ge(s_tr, n + 1)
                dve.tensor_copy(left[:, 2 * n:2 * n + 2].rearrange("p g t -> p (g t)"), bank[n][:]).then_inc(left_done, 1)
            rounds = CAP // 8
            for r in range(rounds):
                at = slice(8 * r, 8 * r + 8)
                dve.wait_ge(left_done, 2 + NG * r)
                for g in range(NG):
                    dve.max(value[:, g, at], left[:, g]).then_inc(top, 1)
                dve.wait_ge(top, NG * (r + 1))
                for g in range(NG):
                    dve.max_index(index[:, g, at], value[:, g, at], left[:, g]).then_inc(found, 1)
                dve.wait_ge(found, NG * (r + 1))
                if r < rounds - 1:
                    for g in range(NG):
                        dve.match_replace(left[:, g], value[:, g, at], left[:, g], -1.0).then_inc(left_done, 1)
            dve.tensor_copy(index_f[:], index[:]).then_inc(as_float, 1)
            dve.wait_ge(i_tr, 1)
            dve.wait_ge(const, Q4)
            for q in range(Q4):
                dve.tensor_tensor(token_of[q * CAP:(q + 1) * CAP].rearrange("c e (g h) -> c g h e", g=NG),
                                  bank[2][0:CAP].rearrange("c (g h q e) -> c q g h e", g=NG, q=Q4, e=E)[:, q],
                                  first_token[:, q].rearrange("c g (h o) -> c g h o", o=1).broadcast_to([CAP, NG, GB // Q4, E]),
                                  ALU.add).then_inc(col_done, 1)
            for q in range(Q4):
                dve.tensor_copy(index_col[q * CAP:(q + 1) * CAP].rearrange("c b k o -> c b (k o)"),
                                bank[2][0:CAP].rearrange("c (b k q) -> c q b k", k=KS, q=Q4)[:, q]).then_inc(col_done, 1)




CHUNK = 512
CHUNKS = B * CAP // CHUNK
XBODY = 2 * CHUNKS
XBODIES = E // 2
TILES = CHUNK // P
WG, WU, WD = slice(0, KC * F), slice(KC * F, 2 * KC * F), slice(2 * KC * F, 2 * KC * F + FT * C)


class ExpertWeights:

    def __init__(self, al):
        self.w_raw = al.sb("w_raw", [P, 2, N_W])
        self.w_hi, self.w_lo = al.split("w", [P, 2, N_W])
        self.w_in = [al.sem(f"w_in{i}") for i in range(2)]
        self.whi_done, self.wlo_done = al.sem("whi_done"), al.sem("wlo_done")
        self.shared = [(al.sb(n + "_raw", [P, k, KC * F // k]), *al.split(n, [P, k, KC * F // k]))
                       for n, k in (("sg", KC), ("su", KC), ("sd", FT))]
        self.shared_in, self.shared_hi = al.sem("shared_in"), al.sem("shared_hi")


def load_expert(sp, ahead, i, d, e):
    for part, name, inner in ((WG, "eg", F), (WU, "eu", F), (WD, "ed", C)):
        sp.dma_start(ahead.w_raw[:, i, part].rearrange("p (k n) -> p k n", n=inner),
                     d[name][e].rearrange("(k p) n -> p k n", p=P)).then_inc(ahead.w_in[i], 16)


def experts(nc, bank, ident, token_of, ahead, d):
    with ExitStack() as ctx:
        al = Alloc(nc, ctx, "ex")
        w_raw, w_hi, w_lo, w_in, whi_done, wlo_done = (
            ahead.w_raw, ahead.w_hi, ahead.w_lo, ahead.w_in, ahead.whi_done, ahead.wlo_done)
        tokens = al.sb("tokens", [P, 2, GATHERS], U32)
        x_raw = al.sb("x_raw", [P, 2, TILES, C])
        x_hi, x_lo = al.split("x", [P, 2, KC, CHUNK])
        act_g = al.sb("act_g", [P, 2, CHUNK])
        hid = al.sb("hid", [P, 2, CHUNK])
        h_hi, h_lo = al.split("h", [P, 2, FT, CHUNK])
        out = al.sb("out", [P, 2, CHUNK // P, C])
        x_in = [al.sem(f"x_in{i}") for i in range(2)]
        stored = [al.sem(f"stored{i}") for i in range(2)]
        xhi_done, xlo_done = al.sem("xhi_done"), al.sem("xlo_done")
        tokens_done, x_tr, spare_pool = al.sem("tokens_done"), al.sem("x_tr"), al.sem("spare_pool")
        g_mm, u_mm, gelu_done, hid_done = al.sem("g_mm"), al.sem("u_mm"), al.sem("gelu_done"), al.sem("hid_done")
        hhi_done, hlo_done = al.sem("hhi_done"), al.sem("hlo_done")
        d_mm, act_out, dve_out = al.sem("d_mm"), al.sem("act_out"), al.sem("dve_out")
        GB, UB, DB, XT = bank[0:2], bank[2:4], bank[4:6], bank[6:8]

        def n_of(J, n, per=1, more=0):
            return J * (XBODY * per) + (per * (n + 1) + more)

        def exists(J, n):
            return not isinstance(J, int) or 0 <= XBODY * J + n < E * CHUNKS

        def weights(t, i, part, inner):
            return t[:, i, part].rearrange("p (k n) -> p k n", n=inner)

        GL, DL = 1, 2

        block = ctx.enter_context(nc.Block())

        @block.sync
        def _(sp):
            def body(J):
                for n in range(XBODY):
                    i, e = n % 2, n // CHUNKS
                    if exists(J, n) and n % CHUNKS == 0 and not (isinstance(J, int) and J == 0):
                        need(sp, wlo_done, J * 2 + (e - 1))
                        load_expert(sp, ahead, e, d, J * 2 + e)
                    m = n - DL - 1
                    if exists(J, m):
                        need(sp, act_out, n_of(J, m))
                        need(sp, dve_out, n_of(J, m))
                        rows = d["eo"][J * 2 + m // CHUNKS].rearrange("b c f -> (b c) f")
                        sp.dma_start(rows[(m % CHUNKS) * CHUNK:(m % CHUNKS + 1) * CHUNK].rearrange("(t p) f -> p t f", p=P),
                                     out[:, m % 2]).then_inc(stored[m % 2], 16)

            over_bodies(sp, body, 1, XBODIES, XBODIES + 1)
            for i in range(2):
                sp.wait_ge(stored[i], 16 * E * CHUNKS // 2)

        @block.gpsimd
        def _(pool):
            def body(J):
                for n in range(XBODY):
                    i, e = n % 2, n // CHUNKS
                    if exists(J, n):
                        if n % CHUNKS == 0:
                            need_alone(pool, x_tr, n_of(J, (e - 1) * CHUNKS - 1), spare_pool)
                            pool.tensor_copy(tokens[:, e], token_of[:, J * 2 + e]).then_inc(tokens_done, 1)
                            need_alone(pool, tokens_done, J * 2 + e + 1, spare_pool)
                        need_alone(pool, x_tr, n_of(J, n - 2), spare_pool)
                        for t in range(TILES):
                            j = (n % CHUNKS) * TILES + t
                            pool.indirect_dma_start(x_raw[:, i, t], None, d["x2"].rearrange("b t c -> (b t) c"),
                                                    bass.IndirectOffsetOnAxis(ap=tokens[:, e, j:j + 1], axis=0)).then_inc(x_in[i], 16)

            over_bodies(pool, body, 1, XBODIES, XBODIES)

        @block.tensor
        def _(pe):
            def body(J):
                for m in range(XBODY):
                    n = m
                    if exists(J, n):
                        i = n % 2
                        need(pe, x_in[i], J * (8 * XBODY * TILES) + 16 * TILES * (n // 2 + 1))
                        need(pe, xlo_done, n_of(J, n - 1))
                        for k in range(KC):
                            for t in range(TILES):
                                mm = pe.transpose(XT[k][:, t * P:t * P + P], x_raw[:, i, t, k * P:k * P + P], ident[:])
                        mm.then_inc(x_tr, 1)
                    n = m - GL
                    if exists(J, n):
                        i, e = n % 2, (n // CHUNKS) % 2
                        need(pe, wlo_done, J * 2 + n // CHUNKS + 1)
                        need(pe, xlo_done, n_of(J, n))
                        wg, wu = [(weights(w_hi, e, part, F), weights(w_lo, e, part, F)) for part in (WG, WU)]
                        for f in range(FT):
                            fs = slice(f * P, f * P + P)
                            need(pe, gelu_done, n_of(J, n, FT, f - FT - 1))
                            for k in range(KC):
                                mm = three(pe, GB[f % 2][:], wg[0][:, k, fs], wg[1][:, k, fs], x_hi[:, i, k], x_lo[:, i, k],
                                           k == 0, k == KC - 1)
                            mm.then_inc(g_mm, 1)
                            need(pe, hid_done, n_of(J, n, FT, f - FT - 1))
                            for k in range(KC):
                                mm = three(pe, UB[f % 2][:], wu[0][:, k, fs], wu[1][:, k, fs], x_hi[:, i, k], x_lo[:, i, k],
                                           k == 0, k == KC - 1)
                            mm.then_inc(u_mm, 1)
                    n = m - DL
                    if exists(J, n):
                        i, e = n % 2, (n // CHUNKS) % 2
                        need(pe, hlo_done, n_of(J, n, FT))
                        need(pe, act_out, n_of(J, n - 1))
                        need(pe, dve_out, n_of(J, n - 1))
                        wd = weights(w_hi, e, WD, C), weights(w_lo, e, WD, C)
                        for t in range(CHUNK // P):
                            ts = slice(t * P, t * P + P)
                            to = DB[t // 2][:, (t % 2) * C:(t % 2) * C + C]
                            for f in range(FT):
                                mm = three(pe, to, h_hi[:, i, f, ts], h_lo[:, i, f, ts], wd[0][:, f], wd[1][:, f], f == 0, f == FT - 1)
                            if t % 2:
                                mm.then_inc(d_mm, 1)

            over_bodies(pe, body, 1, XBODIES, XBODIES + 1)

        @block.scalar
        def _(act):
            def body(J):
                for m in range(XBODY):
                    n = m
                    if exists(J, n):
                        i, e = n % 2, n // CHUNKS
                        if n % CHUNKS == 0 and not (isinstance(J, int) and J == 0):
                            need(act, w_in[e], J * 48 + 48)
                            need(act, d_mm, n_of(J, (e - 1) * CHUNKS - 1, 2))
                            act.activation(w_hi[:, e], w_raw[:, e], ACT.Copy).then_inc(whi_done, 1)
                        need(act, x_tr, n_of(J, n))
                        need(act, u_mm, n_of(J, n - 2, FT))
                        for k in range(KC):
                            ins = act.activation(x_hi[:, i, k], XT[k][:], ACT.Copy)
                        ins.then_inc(xhi_done, 1)
                    n = m - GL
                    if exists(J, n):
                        i = n % 2
                        need(act, d_mm, n_of(J, n - 2, 2))
                        for f in range(FT + 1):
                            if f < FT:
                                need(act, g_mm, n_of(J, n, FT, f - FT + 1))
                                need(act, hid_done, n_of(J, n, FT, f - FT - 1))
                                act.activation(act_g[:, f % 2], GB[f % 2][:], ACT.Gelu).then_inc(gelu_done, 1)
                            if f > 0:
                                need(act, hid_done, n_of(J, n, FT, f - FT))
                                act.activation(h_hi[:, i, f - 1], hid[:, (f - 1) % 2], ACT.Copy).then_inc(hhi_done, 1)
                    n = m - DL
                    if exists(J, n):
                        i = n % 2
                        need(act, d_mm, n_of(J, n, 2, -1))
                        need(act, stored[i], (J * (8 * XBODY) + 16 * (n // 2)))
                        act.activation(out[:, i, 0:2].rearrange("p t f -> p (t f)"), DB[0][:], ACT.Copy).then_inc(act_out, 1)

            over_bodies(act, body, 1, XBODIES, XBODIES + 1)

        @block.vector
        def _(dve):
            def body(J):
                for m in range(XBODY):
                    n = m
                    if exists(J, n):
                        i, e = n % 2, n // CHUNKS
                        if n % CHUNKS == 0 and not (isinstance(J, int) and J == 0):
                            need(dve, whi_done, J * 2 + e + 1)
                            dve.tensor_tensor(w_lo[:, e], w_raw[:, e], f32(w_hi[:, e]), ALU.subtract).then_inc(wlo_done, 1)
                        need(dve, xhi_done, n_of(J, n))
                        for k in range(KC):
                            ins = dve.tensor_tensor(x_lo[:, i, k], XT[k][:], f32(x_hi[:, i, k]), ALU.subtract)
                        ins.then_inc(xlo_done, 1)
                    n = m - GL
                    if exists(J, n):
                        i = n % 2
                        for f in range(FT + 1):
                            if f < FT:
                                need(dve, u_mm, n_of(J, n, FT, f - FT + 1))
                                need(dve, gelu_done, n_of(J, n, FT, f - FT + 1))
                                need(dve, hhi_done, n_of(J, n, FT, f - FT - 1))
                                need(dve, hlo_done, n_of(J, n, FT, f - FT - 1))
                                dve.tensor_tensor(hid[:, f % 2], act_g[:, f % 2], UB[f % 2][:], ALU.mult).then_inc(hid_done, 1)
                            if f > 0:
                                need(dve, hhi_done, n_of(J, n, FT, f - FT))
                                dve.tensor_tensor(h_lo[:, i, f - 1], hid[:, (f - 1) % 2], f32(h_hi[:, i, f - 1]),
                                                  ALU.subtract).then_inc(hlo_done, 1)
                    n = m - DL
                    if exists(J, n):
                        i = n % 2
                        need(dve, d_mm, n_of(J, n, 2))
                        need(dve, stored[i], (J * (8 * XBODY) + 16 * (n // 2)))
                        dve.tensor_copy(out[:, i, 2:4].rearrange("p t f -> p (t f)"), DB[1][:]).then_inc(dve_out, 1)

            over_bodies(dve, body, 1, XBODIES, XBODIES + 1)




def combine(nc, bank, ident, index_col, weight_col, shared, d):
    with ExitStack() as ctx:
        al = Alloc(nc, ctx, "co")
        wg, wu, wd = ((hi, lo) for _, hi, lo in shared)
        token_row = al.sb("token_row", [P, T])
        half = al.sb("half", [P, TT])
        x_raw = al.sb("x_raw", [P, 2, TT, C])
        x_res = al.sb("x_res", [P, TT, C])
        xT_hi, xT_lo = al.split("xT", [P, 2, KC, T])
        eo_raw = al.sb("eo_raw", [P, 2, KS, C])
        eo_hi, eo_lo = al.split("eo", [P, 2, KS, C])
        onehot = al.sb("onehot", [P, 2, KS, T], F32R)
        act_g = al.sb("act_g", [P, 2, 2, T])
        hid = al.sb("hid", [P, 2, 2, T])
        h_hi, h_lo = al.split("h", [P, 2, FT, T])
        res = al.sb("res", [P, TT, C])
        stats, meanvar = al.sb("stats", [P, TT, 6]), al.sb("meanvar", [P, TT, 2])
        var_eps, rstd = al.sb("var_eps", [P, TT]), al.sb("rstd", [P, TT])
        y = al.sb("y", [P, 2, TT, C])
        XT, GB, UB, DB = bank[0], bank[1:3], bank[3:5], bank[5:7]

        const = al.sem("const")
        x_in = [al.sem(f"x_in{i}") for i in range(2)]
        eo_in = [al.sem(f"eo_in{i}") for i in range(2)]
        y_out = [al.sem(f"y_out{i}") for i in range(2)]
        res_in = al.sem("res_in")
        x_tr, xThi_done, xTlo_done = al.sem("x_tr"), al.sem("xThi_done"), al.sem("xTlo_done")
        eohi_done, eolo_done, hot_done = al.sem("eohi_done"), al.sem("eolo_done"), al.sem("hot_done")
        g_mm, u_mm, gelu_done, hid_done = al.sem("g_mm"), al.sem("u_mm"), al.sem("gelu_done"), al.sem("hid_done")
        hhi_done, hlo_done, d_mm, o_read = al.sem("hhi_done"), al.sem("hlo_done"), al.sem("d_mm"), al.sem("o_read")
        st_done, mv_done, ve_done, rstd_done, y_done = (
            al.sem("st_done"), al.sem("mv_done"), al.sem("ve_done"), al.sem("rstd_done"), al.sem("y_done"))
        spare_act, spare_dve = al.sem("spare_act"), al.sem("spare_dve")

        GL, DL, NL = 1, 2, 3
        FP = FT // 2

        block = ctx.enter_context(nc.Block())

        @block.sync
        def _(sp):
            def body(J):
                for i in range(2):
                    if seq_exists(J, i):
                        need(sp, x_tr, upto_seq(J, i - 2))
                        sp.dma_start(x_raw[:, i], d["x2"][J * 2 + i].rearrange("(t p) c -> p t c", p=P)).then_inc(x_in[i], 16)
                        need(sp, eolo_done, upto_seq(J, i - 2, KS))
                        for q in range(P // CAP):
                            sp.dma_start(eo_raw[q * CAP:(q + 1) * CAP, i],
                                         d["eo"].rearrange("(k q) b c f -> q b c k f", k=KS)[q, J * 2 + i]).then_inc(eo_in[i], 16)
                    if seq_exists(J, i - 2):
                        need(sp, o_read, upto_seq(J, i - 3))
                        sp.dma_start(x_res[:], d["x2"][J * 2 + (i - 2)].rearrange("(t p) c -> p t c", p=P)).then_inc(res_in, 16)
                    if seq_exists(J, i - 4):
                        k = i % 2
                        need(sp, y_done, upto_seq(J, i - 4))
                        sp.dma_start(d["out"][J * 2 + (i - 4)].rearrange("(t p) c -> p t c", p=P), y[:, k]).then_inc(y_out[k], 16)

            over_bodies(sp, body, 2, BODIES, BODIES + 2)
            for i in range(2):
                sp.wait_ge(y_out[i], 16 * BODIES)

        @block.gpsimd
        def _(pool):
            pool.iota(token_row[:], pattern=[[1, T]], base=0, channel_multiplier=0,
                      allow_small_or_imprecise_dtypes=True).then_inc(const, 1)
            pool.memset(half[:], -0.5).then_inc(const, 1)
            pool.wait_ge(const, 2)

            def body(J):
                for m in range(2):
                    if seq_exists(J, m - NL):
                        need(pool, ve_done, upto_seq(J, m - NL))
                        pool.tensor_tensor(rstd[:], var_eps[:], half[:], ALU.pow).then_inc(rstd_done, 1)

            over_bodies(pool, body, 2, BODIES, BODIES + 2)

        @block.tensor
        def _(pe):
            def body(J):
                for m in range(2):
                    if seq_exists(J, m):
                        need(pe, x_in[m], J * 16 + 16)
                        need(pe, xTlo_done, upto_seq(J, m - 1))
                        for k in range(KC):
                            for t in range(TT):
                                mm = pe.transpose(XT[:, k * T + t * P:k * T + t * P + P], x_raw[:, m, t, k * P:k * P + P], ident[:])
                        mm.then_inc(x_tr, 1)
                    b = m - GL
                    if seq_exists(J, b):
                        i = b % 2
                        need(pe, xTlo_done, upto_seq(J, b))
                        for fp in range(FP):
                            for to, w, read, mmd in ((GB[fp], wg, gelu_done, g_mm), (UB[fp], wu, hid_done, u_mm)):
                                need(pe, read, upto_seq(J, b - 1, FP, fp - FP + 1))
                                for f in range(2):
                                    fs = slice((2 * fp + f) * P, (2 * fp + f + 1) * P)
                                    for k in range(KC):
                                        mm = three(pe, to[:, f * T:f * T + T], w[0][:, k, fs], w[1][:, k, fs], xT_hi[:, i, k],
                                                   xT_lo[:, i, k], k == 0, k == KC - 1)
                                mm.then_inc(mmd, 1)
                    b = m - DL
                    if seq_exists(J, b):
                        i = b % 2
                        need(pe, hlo_done, upto_seq(J, b, FP))
                        need(pe, hot_done, upto_seq(J, b))
                        need(pe, eolo_done, upto_seq(J, b, KS))
                        need(pe, o_read, upto_seq(J, b - 2))
                        for t in range(TT):
                            ts = slice(t * P, t * P + P)
                            to = DB[i][:, t * C:t * C + C]
                            for f in range(FT):
                                three(pe, to, h_hi[:, i, f, ts], h_lo[:, i, f, ts], wd[0][:, f], wd[1][:, f], f == 0, False)
                            for k in range(KS):
                                pe.matmul(to, onehot[:, i, k, ts], eo_hi[:, i, k], start=False, stop=False, skip_group_check=True)
                                mm = pe.matmul(to, onehot[:, i, k, ts], eo_lo[:, i, k], start=False, stop=k == KS - 1,
                                               skip_group_check=True)
                        mm.then_inc(d_mm, 1)

            over_bodies(pe, body, 2, BODIES, BODIES + 2)

        @block.scalar
        def _(act):
            def body(J):
                for m in range(2):
                    if seq_exists(J, m):
                        need(act, x_tr, upto_seq(J, m))
                        need(act, u_mm, upto_seq(J, m - 2, FP))
                        act.activation(xT_hi[:, m].rearrange("p k t -> p (k t)"), XT[:], ACT.Copy).then_inc(xThi_done, 1)
                    b = m - GL
                    if seq_exists(J, b):
                        i = b % 2
                        for fp in range(FP):
                            need(act, g_mm, upto_seq(J, b, FP, fp - FP + 1))
                            need(act, hid_done, upto_seq(J, b - 1, FP, fp - FP + 1))
                            act.activation(act_g[:, fp].rearrange("p f t -> p (f t)"), GB[fp][:], ACT.Gelu).then_inc(gelu_done, 1)
                        need(act, eo_in[i], J * 64 + 64 * (b // 2 + 1))
                        need_alone(act, d_mm, upto_seq(J, b - 2), spare_act)
                        for k in range(KS):
                            act.activation(eo_hi[:, i, k], eo_raw[:, i, k], ACT.Copy,
                                           scale=weight_col[:, J * 2 + b, k]).then_inc(eohi_done, 1)
                        for fp in range(FP):
                            need(act, hid_done, upto_seq(J, b, FP, fp - FP + 1))
                            act.activation(h_hi[:, i, 2 * fp:2 * fp + 2], hid[:, fp], ACT.Copy).then_inc(hhi_done, 1)

            over_bodies(act, body, 2, BODIES, BODIES + 2)

        @block.vector
        def _(dve):
            dve.wait_ge(const, 2)

            def body(J):
                for m in range(2):
                    if seq_exists(J, m):
                        need(dve, xThi_done, upto_seq(J, m))
                        dve.tensor_tensor(xT_lo[:, m].rearrange("p k t -> p (k t)"), XT[:],
                                          f32(xT_hi[:, m].rearrange("p k t -> p (k t)")), ALU.subtract).then_inc(xTlo_done, 1)
                    b = m - NL
                    if seq_exists(J, b):
                        need(dve, d_mm, upto_seq(J, b))
                        need(dve, res_in, J * 32 + 16 * (b + 1))
                        need(dve, y_done, upto_seq(J, b - 1))
                        dve.tensor_tensor(res[:].rearrange("p t c -> p (t c)"), DB[b % 2][:],
                                          x_res[:].rearrange("p t c -> p (t c)"), ALU.add).then_inc(o_read, 1)
                        need(dve, o_read, upto_seq(J, b))
                        for t in range(TT):
                            dve.bn_stats(stats[:, t], res[:, t]).then_inc(st_done, 1)
                        need_alone(dve, st_done, upto_seq(J, b, TT), spare_dve)
                        for t in range(TT):
                            dve.bn_aggr(meanvar[:, t], stats[:, t]).then_inc(mv_done, 1)
                        need(dve, mv_done, upto_seq(J, b, TT))
                        dve.tensor_scalar(var_eps[:], meanvar[:, :, 1], EPS, None, ALU.add).then_inc(ve_done, 1)
                    b = m - GL
                    if seq_exists(J, b):
                        i = b % 2
                        need(dve, d_mm, upto_seq(J, b - 2))
                        for k in range(KS):
                            ins = dve.tensor_scalar(onehot[:, i, k], token_row[:], index_col[:, J * 2 + b, k], None, ALU.is_equal)
                        ins.then_inc(hot_done, 1)
                        for fp in range(FP):
                            need(dve, u_mm, upto_seq(J, b, FP, fp - FP + 1))
                            need(dve, gelu_done, upto_seq(J, b, FP, fp - FP + 1))
                            need(dve, hhi_done, upto_seq(J, b - 1, FP, fp - FP + 1))
                            need(dve, hlo_done, upto_seq(J, b - 1, FP, fp - FP + 1))
                            dve.tensor_tensor(hid[:, fp].rearrange("p f t -> p (f t)"), act_g[:, fp].rearrange("p f t -> p (f t)"),
                                              UB[fp][:], ALU.mult).then_inc(hid_done, 1)
                        for k in range(KS):
                            need(dve, eohi_done, upto_seq(J, b, KS, k - KS + 1))
                            dve.scalar_tensor_tensor(out=eo_lo[:, i, k], in0=eo_raw[:, i, k], scalar=weight_col[:, J * 2 + b, k],
                                                     in1=f32(eo_hi[:, i, k]), op0=ALU.mult, op1=ALU.subtract).then_inc(eolo_done, 1)
                        for fp in range(FP):
                            need(dve, hhi_done, upto_seq(J, b, FP, fp - FP + 1))
                            dve.tensor_tensor(h_lo[:, i, 2 * fp:2 * fp + 2], hid[:, fp], f32(h_hi[:, i, 2 * fp:2 * fp + 2]),
                                              ALU.subtract).then_inc(hlo_done, 1)
                    b = m - NL
                    if seq_exists(J, b):
                        need(dve, rstd_done, upto_seq(J, b))
                        need(dve, y_out[b % 2], J * 16 + 16 * (b // 2))
                        for t in range(TT):
                            ins = dve.tensor_scalar(y[:, b % 2, t], res[:, t], meanvar[:, t, 0:1], rstd[:, t:t + 1],
                                                    ALU.subtract, ALU.mult)
                        ins.then_inc(y_done, 1)

            over_bodies(dve, body, 2, BODIES, BODIES + 2)


def program(nc, d):
    with ExitStack() as ctx:
        al = Alloc(nc, ctx, "all")
        bank = [ctx.enter_context(nc.psum_tensor(f"bank{i}", [P, 512], F32)) for i in range(8)]
        ident = al.sb("ident", [P, P])
        logits = al.sb("logits", [P, B, TT, E])
        token_of = al.sb("token_of", [P, E, GATHERS], U32)
        index_col = al.sb("index_col", [P, B, KS, 1])
        weight_col = al.sb("weight_col", [P, B, KS, 1])
        made = al.sem("made")
        with nc.Block() as block:
            @block.gpsimd
            def _(pool):
                pool.memset(ident[:], 0.0).then_inc(made, 1)
                pool.wait_ge(made, 1)
                pool.affine_select(out=ident[:], in_=ident[:], compare_op=ALU.not_equal, fill=1.0, base=0,
                                   pattern=[[-1, P]], channel_multiplier=1).then_inc(made, 1)
                pool.wait_ge(made, 2)
        with ExitStack() as attention:
            early = Alloc(nc, attention, "early")
            wv_raw, wv_in = early.sb("wv_raw", [P, KC, H * DH]), early.sem("wv_in")
            self_attention(nc, bank, ident, wv_raw, wv_in, d)
            cross_attention(nc, bank, ident, logits, wv_raw, wv_in, d)
        with ExitStack() as moe:
            ahead = ExpertWeights(Alloc(nc, moe, "ahead"))
            route(nc, bank, ident, logits, index_col, weight_col, token_of, ahead, d)
            experts(nc, bank, ident, token_of, ahead, d)
            combine(nc, bank, ident, index_col, weight_col, ahead.shared, d)




def kernel(**inputs):
    import concourse.bacc as bacc
    from concourse.bass_utils import run_bass_kernel_spmd

    def a(name):
        return np.asarray(inputs[name])

    def t(name):
        return np.swapaxes(a(name), -1, -2)

    def again(v, axis):
        return np.concatenate((v, np.take(v, range(REST, L), axis)), axis)

    ow = a("L0_attn_out_w").reshape(H, L, C).transpose(1, 0, 2).reshape(L, H * C)
    laid = {
        "x": a("x"), "xT": t("x"), "ctxT": t("ctx_1024"),
        "wd": again(a("L0_attn_Wd_w").transpose(1, 0, 2), 2).reshape(C, H * P),
        "lw": again(a("L0_attn_latent_w"), 1),
        "ow_a": again(ow, 0),
        "ow_b": np.concatenate((ow, np.zeros((AT - L, H * C), ow.dtype), ow[:REST], np.zeros((P - AT - REST, H * C), ow.dtype))),
        "qbias": again(t("L0_attn_Wd_b"), 0), "lbias": again(a("L0_attn_latent_b").reshape(L, 1), 0),
        "obias": np.broadcast_to(a("L0_attn_out_b"), (P, C)),
        "wq": a("L0_xattn_Wq").reshape(C, H * DH), "wk": a("L0_xattn_Wk").reshape(C, H * DH),
        "wv": a("L0_xattn_Wv").reshape(C, H * DH),
        "wo": a("L0_xattn_Wo").reshape(NP, P, C).transpose(1, 0, 2).reshape(P, NP * C),
        "gate": t("L0_ffn_gate_w"),
        "eg": t("L0_ffn_Wg"), "eu": t("L0_ffn_Wu"), "ed": t("L0_ffn_Wd"),
        "sg": t("L0_ffn_Ws_g"), "su": t("L0_ffn_Ws_u"), "sd": t("L0_ffn_Ws_d"),
    }
    nc = bacc.Bacc("TRN2", target_bir_lowering=False, num_devices=1)
    arrays, d = {}, {}
    for name, v in laid.items():
        arrays[f"in_{name}"] = np.ascontiguousarray(v)
        d[name] = nc.dram_tensor(f"in_{name}", v.shape, F32, kind="ExternalInput").ap()
    for name, shape, dt in (("x1", (B, T, C), F32), ("x2", (B, T, C), F32), ("eo", (E, B, CAP, C), F32)):
        d[name] = nc.dram_tensor(f"mid_{name}", shape, dt, kind="Internal").ap()
    d["out"] = nc.dram_tensor("out", (B, T, C), F32, kind="ExternalOutput").ap()
    program(nc, d)
    return run_bass_kernel_spmd(nc, [arrays], core_ids=[0]).results[0]["out"]
```
